# Optimizing a Trainium2 kernel written in Bass

```python
import numpy as np
import jax
import jax.numpy as jnp

def _softmax(x, axis=-1):
    return jax.nn.softmax(x, axis=axis)

def _gelu(x):
    return jax.nn.gelu(x, approximate=True)

def _silu(x):
    return jax.nn.silu(x)

def _sigmoid(x):
    return jax.nn.sigmoid(x)

def _layernorm(x, axis=-1, eps=1e-05):
    m = jnp.mean(x, axis=axis, keepdims=True)
    v = jnp.var(x, axis=axis, keepdims=True)
    return (x - m) / jnp.sqrt(v + eps)

def _scatter_add(tgt, idx, src, axis=0):
    return tgt.at[idx].add(src)

def _segment_sum(src, seg, n):
    return jax.ops.segment_sum(src, seg, n)
kernel_name = 'mk_gnn_resnorm_d1_gnn_r8_718a2d'

def setup_inputs(seed: int=0):
    np.random.seed(seed)
    _w = jnp.asarray

    def _rec_inputs():
        import jax
        import jax.numpy as jnp
        _gk = jax.random.key(seed)
        x = -0.0005121 + 1.001 * jax.random.normal(jax.random.fold_in(_gk, 1), (6250, 64), jnp.float32)
        _s = jax.random.randint(jax.random.fold_in(_gk, 2), (100000,), 0, 6250, jnp.int32)
        _d = jax.random.randint(jax.random.fold_in(_gk, 3), (100000,), 0, 6250, jnp.int32)
        _loop = jnp.arange(6250, dtype=jnp.int32)
        src = jnp.concatenate([_s, _d, _loop])
        dst = jnp.concatenate([_d, _s, _loop])
        _o = jnp.argsort(dst, stable=True)
        src = src[_o]
        dst = dst[_o]
        edge_attr_64 = -9.77346e-05 + 0.999888 * jax.random.normal(jax.random.fold_in(_gk, 11), (206250, 64), jnp.float32)
        return (x, src, dst, edge_attr_64)
    x, src, dst, edge_attr_64 = _rec_inputs()

    def _L0_gnn_setup():
        import jax, jax.numpy as jnp
        import numpy as np
        N = 6250
        E = 100000
        D = 64
        L = 3
        LN_EPS = 1e-05

        def _transformer_conv(x, src, dst, edge_attr, Wq, bq, Wk, bk, Wv, bv, We, Ws, bs):
            q = x @ Wq + bq
            k = x @ Wk + bk
            v = x @ Wv + bv
            e = edge_attr @ We
            kj = k[src] + e
            alpha = jnp.sum(q[dst] * kj, axis=-1) / jnp.sqrt(jnp.float32(D))
            amax = jax.ops.segment_max(alpha, dst, num_segments=N)
            p = jnp.exp(alpha - amax[dst])
            denom = jax.ops.segment_sum(p, dst, num_segments=N)
            w = p / denom[dst]
            msg = (v[src] + e) * w[:, None]
            agg = jax.ops.segment_sum(msg, dst, num_segments=N)
            return agg + x @ Ws + bs

        def _layer_norm(x, gamma, beta):
            mu = jnp.mean(x, axis=-1, keepdims=True)
            var = jnp.mean(jnp.square(x - mu), axis=-1, keepdims=True)
            return (x - mu) * jax.lax.rsqrt(var + LN_EPS) * gamma + beta
        key = jax.random.key(seed)
        ks = jax.random.split(key, 16)
        s = 1.0 / np.sqrt(D)
        node_attr = jax.random.normal(ks[0], (N, D), dtype=jnp.float32)
        edge_attr = jax.random.normal(ks[1], (E, D), dtype=jnp.float32)
        edge_index = jax.random.randint(ks[2], (2, E), 0, N, dtype=jnp.int32)
        mk = lambda k: jax.random.normal(k, (L, D, D), dtype=jnp.float32) * s
        return {'node_attr': node_attr, 'edge_index': edge_index, 'edge_attr': edge_attr, 'Wq': mk(ks[3]), 'bq': jnp.zeros((L, D), jnp.float32), 'Wk': mk(ks[4]), 'bk': jnp.zeros((L, D), jnp.float32), 'Wv': mk(ks[5]), 'bv': jnp.zeros((L, D), jnp.float32), 'We': mk(ks[6]), 'Ws': mk(ks[7]), 'bs': jnp.zeros((L, D), jnp.float32), 'ln_gamma': jnp.ones((L - 1, D), jnp.float32), 'ln_beta': jnp.zeros((L - 1, D), jnp.float32)}
    _L0_gnn_all = _L0_gnn_setup()
    _L0_gnn_in = {k: v for k, v in _L0_gnn_all.items() if k in ('Wq', 'bq', 'Wk', 'bk', 'Wv', 'bv', 'We', 'Ws', 'bs', 'ln_gamma', 'ln_beta')}
    del _L0_gnn_all
    return {'x': x, 'src': src, 'dst': dst, 'edge_attr_64': edge_attr_64, 'L0_gnn_Wq': _L0_gnn_in['Wq'], 'L0_gnn_bq': _L0_gnn_in['bq'], 'L0_gnn_Wk': _L0_gnn_in['Wk'], 'L0_gnn_bk': _L0_gnn_in['bk'], 'L0_gnn_Wv': _L0_gnn_in['Wv'], 'L0_gnn_bv': _L0_gnn_in['bv'], 'L0_gnn_We': _L0_gnn_in['We'], 'L0_gnn_Ws': _L0_gnn_in['Ws'], 'L0_gnn_bs': _L0_gnn_in['bs'], 'L0_gnn_ln_gamma': _L0_gnn_in['ln_gamma'], 'L0_gnn_ln_beta': _L0_gnn_in['ln_beta']}

def reference(x, src, dst, edge_attr_64, L0_gnn_Wq, L0_gnn_bq, L0_gnn_Wk, L0_gnn_bk, L0_gnn_Wv, L0_gnn_bv, L0_gnn_We, L0_gnn_Ws, L0_gnn_bs, L0_gnn_ln_gamma, L0_gnn_ln_beta):
    import jax
    import jax.numpy as jnp

    def _L0_gnn_ref(node_attr, edge_index, edge_attr, Wq, bq, Wk, bk, Wv, bv, We, Ws, bs, ln_gamma, ln_beta):
        import jax, jax.numpy as jnp
        import numpy as np
        N = 6250
        E = 100000
        D = 64
        L = 3
        LN_EPS = 1e-05

        def _transformer_conv(x, src, dst, edge_attr, Wq, bq, Wk, bk, Wv, bv, We, Ws, bs):
            q = x @ Wq + bq
            k = x @ Wk + bk
            v = x @ Wv + bv
            e = edge_attr @ We
            kj = k[src] + e
            alpha = jnp.sum(q[dst] * kj, axis=-1) / jnp.sqrt(jnp.float32(D))
            amax = jax.ops.segment_max(alpha, dst, num_segments=N)
            p = jnp.exp(alpha - amax[dst])
            denom = jax.ops.segment_sum(p, dst, num_segments=N)
            w = p / denom[dst]
            msg = (v[src] + e) * w[:, None]
            agg = jax.ops.segment_sum(msg, dst, num_segments=N)
            return agg + x @ Ws + bs

        def _layer_norm(x, gamma, beta):
            mu = jnp.mean(x, axis=-1, keepdims=True)
            var = jnp.mean(jnp.square(x - mu), axis=-1, keepdims=True)
            return (x - mu) * jax.lax.rsqrt(var + LN_EPS) * gamma + beta
        src, dst = (edge_index[0], edge_index[1])
        x = node_attr
        for i in range(L):
            x = _transformer_conv(x, src, dst, edge_attr, Wq[i], bq[i], Wk[i], bk[i], Wv[i], bv[i], We[i], Ws[i], bs[i])
            x = jax.nn.relu(x)
            if i < L - 1:
                x = _layer_norm(x, ln_gamma[i], ln_beta[i])
        return jax.nn.log_softmax(x, axis=1)
    edge_index = jnp.stack([src, dst])
    x = _layernorm(x + _L0_gnn_ref(x, edge_index, edge_attr_64, L0_gnn_Wq, L0_gnn_bq, L0_gnn_Wk, L0_gnn_bk, L0_gnn_Wv, L0_gnn_bv, L0_gnn_We, L0_gnn_Ws, L0_gnn_bs, L0_gnn_ln_gamma, L0_gnn_ln_beta), axis=-1)
    return x

_drawn_inputs = setup_inputs


def setup_inputs(seed=0):
    import zlib

    import numpy as np

    out = dict(_drawn_inputs(seed))
    spreads = {'L0_gnn_bq': (0.0, 0.1),
     'L0_gnn_bk': (0.0, 0.1),
     'L0_gnn_bv': (0.0, 0.1),
     'L0_gnn_bs': (0.0, 0.1),
     'L0_gnn_ln_gamma': (1.0, 0.2),
     'L0_gnn_ln_beta': (0.0, 0.1)}
    factors = {}
    for name, (base, spread) in spreads.items():
        noise = np.random.default_rng([zlib.crc32(name.encode()), seed]).standard_normal(out[name].shape)
        drawn = base * np.exp(spread * noise) if base else spread * noise
        out[name] = jnp.asarray(drawn.astype(out[name].dtype))
    for name, factor in factors.items():
        out[name] = (out[name] * factor).astype(out[name].dtype)
    return out
```

```python
from contextlib import ExitStack

import concourse.bass as bass
from concourse import mybir

F32 = mybir.dt.float32
BF16 = mybir.dt.bfloat16
I32 = mybir.dt.int32
ALU = mybir.AluOpType
ACT = mybir.ActivationFunctionType
AX = mybir.AxisListType

N, E, D, L = 6250, 206250, 64, 3
P = 128
T = 13
EC = T * P
SLOTS = 4
GROUPS = -(-E // (EC * SLOTS))
C = GROUPS * SLOTS
W = 64
NWIN = -(-N // W)
U0B = 4
U0N = -(-(N + W) // (U0B * P))
NP = U0N * U0B * P
PAD_DST = 1 << 20
F2 = 2 * D
UC = F2 + 1
FP = 3 * D
UW = UC + D
SC = UC + 1
UPITCH = 160
BIG = 3.0e38
M_INIT = -1.5e38
LN_EPS = 1e-5
FORCE_GENERAL = 0


def gnn_kernel(nc, x, xT, src, dst, edge, w_qT, w_ke, w_sk, w_ve, w_vec, out, x_table, u_table):
    with ExitStack() as ctx:
        def sb(name, shape, dt=F32):
            return ctx.enter_context(nc.sbuf_tensor(name, shape, dt))

        def ps(name, shape, dt=F32):
            return ctx.enter_context(nc.psum_tensor(name, shape, dt))

        def sem(name):
            return ctx.enter_context(nc.semaphore(name))

        dst_i = sb("dst_i", [P, (C + 1) * T], I32)
        dst_f = sb("dst_f", [P, (C + 1) * T])
        src_l = sb("src_l", [P, L * C * T], I32)
        base_b = sb("base_b", [P, C + 1])
        step_b = sb("step_b", [P, C])
        wbase = sb("wbase", [P, NWIN])
        sel_all = sb("sel_all", [W + 1, C])
        diag_i = sb("diag_i", [P, P], I32)
        iota_i = sb("iota_i", [P, P], I32)
        iota_n = sb("iota_n", [P, P])
        ident = sb("ident", [P, P])
        ident_b = sb("ident_b", [P, P], BF16)
        row_id = sb("row_id", [P, 1])
        ones = sb("ones", [P, P])
        eps_t = sb("eps_t", [P, 1])
        xT1 = sb("xT1", [D + 1, NP])
        qT_sb = sb("qT_sb", [D, L, D + 1])
        ke_sb = sb("ke_sb", [D, L, UC])
        g_all = sb("g_all", [D + 1, L, UW])
        ve_all = sb("ve_all", [F2, L, D])
        vec_all = sb("vec_all", [W, L, 3 * D])
        far = sb("far", [P, C, T])
        wide = sb("wide", [P, C, T])
        lim = sb("lim", [P, C])
        bad = sb("bad", [P, 4])
        bad_n = sb("bad_n", [P, 1])
        flag_f = sb("flag_f", [1, 1])
        flag_i = sb("flag_i", [1, 1], I32)
        g_next = sb("g_next", [D + 1, UW])
        ve_cur = sb("ve_cur", [F2, D])
        vec_cur = sb("vec_cur", [W, 3 * D])
        feat = [sb(f"feat{s}", [P, T, FP]) for s in range(SLOTS)]
        idx = [sb(f"idx{s}", [P, T], I32) for s in range(SLOTS)]
        u_win = [sb(f"u_win{s}", [P, UW]) for s in range(SLOTS)]
        x0 = [sb(f"x0{s}", [W, D]) for s in range(SLOTS)]
        xnew = [sb(f"xnew{s}", [W, D]) for s in range(SLOTS)]
        u_out = [sb(f"u_out{s}", [W, UW]) for s in range(SLOTS)]
        rel = sb("rel", [P, T])
        ne = [sb(f"ne{k}", [P, T, W], BF16) for k in range(2)]
        mT = sb("mT", [P, (T + 1) // 2, P])
        dot_out = sb("dot_out", [P, T, UC], BF16)
        alpha = sb("alpha", [P, T])
        score = sb("score", [P, T, W])
        prob = sb("prob", [P, T, W])
        cmax = sb("cmax", [P, W])
        cm = sb("cm", [W, 1])
        m_new = sb("m_new", [W, 1])
        diag = sb("diag", [W, W])
        sel = sb("sel", [W + 1, 1])
        old = sb("old", [1, SC])
        m_dif = sb("m_dif", [W, 1])
        m_fac = sb("m_fac", [W, 1])
        state = [sb(f"state{k}", [W + 1, SC]) for k in range(2)]
        d_pos = sb("d_pos", [W, 1])
        d_inv = sb("d_inv", [W, 1])
        some = sb("some", [W, 1])
        skip = sb("skip", [W, D])
        aggT = sb("aggT", [F2, W])
        xo = sb("xo", [W, D])
        xr = sb("xr", [W, D])
        bns = sb("bns", [W, 6])
        mv = sb("mv", [W, 2])
        lnv = sb("lnv", [W, 1])
        rstd = sb("rstd", [W, 1])
        xn = sb("xn", [W, D])
        xnT = sb("xnT", [D + 1, W])
        mx = sb("mx", [W, 1])
        mneg = sb("mneg", [W, 1])
        ex = sb("ex", [W, D])
        esum = sb("esum", [W, 1])
        lse = sb("lse", [W, 1])
        shift = sb("shift", [W, 1])
        big = sb("big", [P, max(U0N * U0B * UW, NWIN * SC)])
        u0_out = big[:, 0:U0N * U0B * UW].rearrange("p (b f) -> p b f", f=UW)
        all_flat = big[0:W, 0:NWIN * SC]
        all_state = all_flat.rearrange("p (w f) -> p w f", f=SC)

        u_ps = ps("u_ps", [P, 6, 512])
        neT_ps = u_ps[:, 5, :].bitcast(BF16).rearrange("p (j e) -> p j e", e=P)
        max_ps = ps("max_ps", [P, 512])
        agg_ps = ps("agg_ps", [P, 512])
        cmT = max_ps[0:W, 0:P]
        m_bc = max_ps[:, P:P + W]
        xnT_ps = max_ps[0:D, P + W:P + 2 * W]
        uo_ps = max_ps[0:W, 2 * P:2 * P + UW]
        agg = agg_ps[0:W, 0:UC]
        o_ps = agg_ps[0:W, 136:136 + D]
        aggT_ps = agg_ps[:, 200:200 + W]
        old_ps = agg_ps[0:1, 264:264 + SC]

        def u_slot(t):
            j = t // 2
            return u_ps[:, 3 * (t % 2) + j // 3, (j % 3) * UPITCH:(j % 3) * UPITCH + UC]

        src_loaded = sem("src_loaded")
        dst_loaded = sem("dst_loaded")
        weights_loaded = sem("weights_loaded")
        x_filled = sem("x_filled")
        iota_ready = sem("iota_ready")
        const_ready = sem("const_ready")
        dst_ready = sem("dst_ready")
        base_mm = sem("base_mm")
        base_ready = sem("base_ready")
        test_step = sem("test_step")
        bad_ready = sem("bad_ready")
        bad_mm = sem("bad_mm")
        flag_ready = sem("flag_ready")
        g_mm = sem("g_mm")
        g_ready = sem("g_ready")
        u0_mm = sem("u0_mm")
        u0_copied = sem("u0_copied")
        x_stored = sem("x_stored")
        u_stored = sem("u_stored")
        out_stored = sem("out_stored")
        layer_stored = sem("layer_stored")
        layer_w = sem("layer_w")
        edge_loaded = [sem(f"edge_loaded{s}") for s in range(SLOTS)]
        rows_loaded = [sem(f"rows_loaded{s}") for s in range(SLOTS)]
        uwin_loaded = [sem(f"uwin_loaded{s}") for s in range(SLOTS)]
        x0_loaded = [sem(f"x0_loaded{s}") for s in range(SLOTS)]
        idx_ready = sem("idx_ready")
        rel_ready = sem("rel_ready")
        ne_ready = sem("ne_ready")
        neT_done = sem("neT_done")
        mT_ready = sem("mT_ready")
        u_gathered = sem("u_gathered")
        dots_done = sem("dots_done")
        score_ready = sem("score_ready")
        cmax_ready = sem("cmax_ready")
        cmT_done = sem("cmT_done")
        cm_ready = sem("cm_ready")
        sel_ready = sem("sel_ready")
        old_done = sem("old_done")
        old_ready = sem("old_ready")
        m_ready = sem("m_ready")
        mdif_ready = sem("mdif_ready")
        mfac_ready = sem("mfac_ready")
        diag_ready = sem("diag_ready")
        m_bc_done = sem("m_bc_done")
        shifted = sem("shifted")
        prob_ready = sem("prob_ready")
        agg_done = sem("agg_done")
        sums_copied = sem("sums_copied")
        merged = sem("merged")
        aggT_done = sem("aggT_done")
        aggT_ready = sem("aggT_ready")
        dpos_ready = sem("dpos_ready")
        dinv_ready = sem("dinv_ready")
        some_ready = sem("some_ready")
        skip_ready = sem("skip_ready")
        o_done = sem("o_done")
        xo_ready = sem("xo_ready")
        xr_ready = sem("xr_ready")
        bns_ready = sem("bns_ready")
        mv_ready = sem("mv_ready")
        lnv_ready = sem("lnv_ready")
        rstd_ready = sem("rstd_ready")
        xn_ready = sem("xn_ready")
        xnew_ready = sem("xnew_ready")
        xnT_done = sem("xnT_done")
        xnT_ready = sem("xnT_ready")
        uo_done = sem("uo_done")
        uo_ready = sem("uo_ready")
        mx_ready = sem("mx_ready")
        mneg_ready = sem("mneg_ready")
        ex_ready = sem("ex_ready")
        lse_ready = sem("lse_ready")
        shift_ready = sem("shift_ready")
        logp_ready = sem("logp_ready")
        res_bns = sem("res_bns")
        res_mv = sem("res_mv")
        res_lnv = sem("res_lnv")
        res_rstd = sem("res_rstd")
        res_ready = sem("res_ready")
        sp_mark = sem("sp_mark")
        pool_mark = sem("pool_mark")
        pe_mark = sem("pe_mark")
        dve_mark = sem("dve_mark")
        win_free = sem("win_free")
        win_landed = sem("win_landed")
        win_loaded = sem("win_loaded")
        rows_stored = sem("rows_stored")
        rows_kept = sem("rows_kept")
        window_merged = sem("window_merged")
        state_set = sem("state_set")
        state_got = sem("state_got")

        N_WEIGHTS = 6
        STEPS = C * NWIN + NWIN
        block = ctx.enter_context(nc.Block())

        def rows(table, row):
            return table[bass.ds(row, W), :]

        @block.sync
        def _(sp):
            sp.dma_start(src_l[:, 0:C * T], src).then_inc(src_loaded, 16)
            sp.dma_start(dst_i[:], dst).then_inc(dst_loaded, 16)
            sp.dma_start(qT_sb[:], w_qT).then_inc(weights_loaded, 16)
            sp.dma_start(ke_sb[:], w_ke).then_inc(weights_loaded, 16)
            sp.dma_start(g_all[:, :, UC:UW], w_sk).then_inc(weights_loaded, 16)
            sp.dma_start(xT1[0:D, :], xT).then_inc(weights_loaded, 16)
            sp.dma_start(ve_all[:], w_ve).then_inc(weights_loaded, 16)
            sp.dma_start(vec_all[:], w_vec).then_inc(weights_loaded, 16)

            def load_edges(c, s):
                e = edge[bass.ds(c, 1), :, :].rearrange("a p (t d) -> (a p) t d", d=D)
                sp.dma_start(feat[s][:, :, D:F2], e).then_inc(edge_loaded[s], 16)

            def load(l, c, s, last):
                node = sp.value_load(dst_i[0:1, bass.ds(c * T, 1)], min_val=0, max_val=N - 1)
                load_edges(c, s)
                for h in range(2):
                    sp.dma_start(u_win[s][h * W:(h + 1) * W, :], rows(u_table, l * NP + node)).then_inc(uwin_loaded[s], 16)
                if last:
                    sp.dma_start(x0[s][:], rows(x, node)).then_inc(x0_loaded[s], 16)

            def store(l, c, s, last):
                node = sp.value_load(dst_i[0:1, bass.ds(c * T, 1)], min_val=0, max_val=N - 1)
                if last:
                    c1 = sp.snap(c + 1)
                    sp.wait_ge(res_ready, c1)
                    sp.dma_start(rows(out, node), xnew[s][:]).then_inc(out_stored, 16)
                    sp.wait_ge(out_stored, 16 * c1)
                else:
                    n = sp.snap(l * C + c)
                    x_row = sp.snap(l * NP + node)
                    u_row = sp.snap((l + 1) * NP + node)
                    sp.wait_ge(uo_ready, n + 1)
                    sp.dma_start(rows(x_table, x_row), xnew[s][:]).then_inc(x_stored, 16)
                    sp.dma_start(rows(u_table, u_row), u_out[s][:]).then_inc(u_stored, 16)
                    sp.wait_ge(x_stored, 16 * (n + 1))
                    sp.wait_ge(u_stored, 16 * (n + 1 + U0N))
                sp.sem_inc(sp_mark, 1)

            def sorted_layer(l, last):
                for s in range(SLOTS):
                    load(l, s, s, last)
                with sp.Fori(1, GROUPS) as g:
                    for s in range(SLOTS):
                        store(l, (g - 1) * SLOTS + s, s, last)
                        load(l, g * SLOTS + s, s, last)
                for s in range(SLOTS):
                    store(l, C - SLOTS + s, s, last)
                sp.sem_inc(layer_stored, 1)

            def load_window(row, j):
                sp.wait_ge(win_free, j + 1)
                sp.sem_inc(sp_mark, 1)
                for h in range(2):
                    sp.dma_start(u_win[0][h * W:(h + 1) * W, :], rows(u_table, row)).then_inc(win_landed, 16)
                sp.wait_ge(win_landed, 32)
                sp.sem_clear(win_landed)
                sp.sem_inc(win_loaded, 1)

            def general_layer(l, last):
                with sp.Fori(0, GROUPS) as g:
                    for s in range(SLOTS):
                        c = sp.snap(g * SLOTS + s)
                        load_edges(c, s)
                        with sp.Fori(0, NWIN) as w:
                            load_window(l * NP + w * W, l * STEPS + c * NWIN + w)
                with sp.Fori(0, NWIN) as w:
                    n = sp.snap(l * NWIN + w)
                    row = sp.snap(w * W)
                    if last:
                        sp.dma_start(x0[0][:], rows(x, row)).then_inc(rows_stored, 16)
                        sp.wait_ge(rows_stored, 16)
                        sp.sem_clear(rows_stored)
                    load_window(l * NP + row, l * STEPS + C * NWIN + w)
                    if last:
                        sp.wait_ge(res_ready, w + 1)
                        sp.dma_start(rows(out, row), xnew[0][:]).then_inc(rows_stored, 16)
                        sp.wait_ge(rows_stored, 16)
                    else:
                        x_row = sp.snap(l * NP + row)
                        u_row = sp.snap((l + 1) * NP + row)
                        sp.wait_ge(uo_ready, n + 1)
                        sp.dma_start(rows(x_table, x_row), xnew[0][:]).then_inc(rows_stored, 16)
                        sp.dma_start(rows(u_table, u_row), u_out[0][:]).then_inc(rows_stored, 16)
                        sp.wait_ge(rows_stored, 32)
                    sp.sem_clear(rows_stored)
                    sp.sem_inc(rows_kept, 1)
                sp.sem_inc(layer_stored, 1)

            for i in range(U0N):
                sp.wait_ge(u0_copied, i + 1)
                r = u_table[i * U0B * P:(i + 1) * U0B * P, :].rearrange("(b p) f -> p b f", p=P)
                sp.dma_start(r, u0_out[:, i * U0B:(i + 1) * U0B, :]).then_inc(u_stored, 16)
            for l in range(L - 1):
                sp.dma_start(x_table[l * NP:(l + 1) * NP, :], x).then_inc(x_filled, 16)
            sp.wait_ge(u_stored, 16 * U0N)
            sp.wait_ge(x_filled, 16 * (L - 1))
            sp.wait_ge(flag_ready, 1)
            general = sp.value_load(flag_i[:], min_val=0, max_val=1)
            with sp.If(general):
                with sp.Fori(0, L - 1) as l:
                    general_layer(l, False)
                general_layer(L - 1, True)
            with sp.Else():
                with sp.Fori(0, L - 1) as l:
                    sorted_layer(l, False)
                sorted_layer(L - 1, True)
                sp.wait_ge(out_stored, 16 * C)
                sp.wait_ge(x_stored, 16 * (L - 1) * C)
                sp.wait_ge(u_stored, 16 * ((L - 1) * C + U0N))

        @block.gpsimd
        def _(pool):
            nc.gpsimd.iota(iota_i[:], pattern=[[1, P]], base=0, channel_multiplier=0).then_inc(iota_ready, 1)
            nc.gpsimd.iota(diag_i[:], pattern=[[1, P]], base=0, channel_multiplier=-1).then_inc(iota_ready, 1)

            def gather(table, n1, s):
                pool.wait_ge(idx_ready, n1)
                pool.sem_inc(pool_mark, 1)
                for t in range(T):
                    nc.gpsimd.indirect_dma_start(
                        feat[s][:, t, 0:D], None, table, bass.IndirectOffsetOnAxis(idx[s][:, t:t + 1], 0),
                    ).then_inc(rows_loaded[s], 16)

            def layer(table, l):
                for s in range(SLOTS):
                    gather(table, l * C + s + 1, s)
                with pool.Fori(1, GROUPS) as g:
                    for s in range(SLOTS):
                        n1 = pool.snap((l * C + s + 1) + g * SLOTS)
                        pool.wait_ge(merged, n1 - SLOTS)
                        gather(table, n1, s)

            layer(x, 0)
            with pool.Fori(1, L) as l:
                pool.wait_ge(layer_stored, l)
                layer(x_table, l)

        @block.scalar
        def _(act):
            nc.scalar.preload_act_table_set("natural_log_exp_and_others")
            for l in range(L):
                act.wait_ge(g_mm, l + 1)
                act.wait_ge(weights_loaded, 16 * N_WEIGHTS)
                nc.scalar.activation(g_all[:, l, 0:UC], u_ps[0:D + 1, l, 0:UC], ACT.Copy, scale=D ** -0.5).then_inc(g_ready, 1)
            for i in range(U0N):
                act.wait_ge(u0_mm, i + 1)
                for h in range(2):
                    u2 = u_ps[:, 2 * (i % 2) + h, :].rearrange("p (b f) -> p b f", b=2)[:, :, 0:UW]
                    ins = nc.scalar.copy(u0_out[:, i * U0B + 2 * h:i * U0B + 2 * h + 2, :], u2)
                ins.then_inc(u0_copied, 1)

            def mask_rows(n1):
                act.wait_ge(neT_done, n1)
                nc.scalar.activation(mT[:, 0:T // 2, :], neT_ps[:, 0:T // 2, :], ACT.Copy, scale=-1.0, bias=1.0)
                nc.scalar.activation(mT[0:W, T // 2, :], neT_ps[0:W, T // 2, :], ACT.Copy, scale=-1.0,
                                     bias=1.0).then_inc(mT_ready, 1)

            def copy_sums(k, n1):
                act.wait_ge(agg_done, n1)
                nc.scalar.copy(state[k][0:W, 0:UC], agg).then_inc(sums_copied, 1)

            def factor(m, n1):
                act.wait_ge(mdif_ready, n1)
                nc.scalar.activation(m_fac[0:m, :], m_dif[0:m, :], ACT.Exp).then_inc(mfac_ready, 1)

            def exponentials(n1):
                act.wait_ge(shifted, n1)
                nc.scalar.activation(prob[:], score[:], ACT.Exp).then_inc(prob_ready, 1)

            def copy_aggT(n1):
                act.wait_ge(aggT_done, n1)
                nc.scalar.copy(aggT[:], aggT_ps).then_inc(aggT_ready, 1)

            def inverse_std(n1, mv_done, ln_done, done):
                act.wait_ge(mv_done, n1)
                nc.scalar.activation(lnv[:], mv[:, 1:2], ACT.Ln, bias=eps_t[0:W, :]).then_inc(ln_done, 1)
                act.wait_ge(ln_done, n1)
                nc.scalar.activation(rstd[:], lnv[:], ACT.Exp, scale=-0.5).then_inc(done, 1)

            def node_std(n1, c1, last):
                if last:
                    act.wait_ge(mneg_ready, c1)
                    nc.scalar.activation(ex[:], xr[:], ACT.Exp, bias=mneg[:], accum_out=esum[:]).then_inc(ex_ready, 1)
                    act.wait_ge(ex_ready, c1)
                    nc.scalar.activation(lse[:], esum[:], ACT.Ln).then_inc(lse_ready, 1)
                    inverse_std(c1, res_mv, res_lnv, res_rstd)
                else:
                    inverse_std(n1, mv_ready, lnv_ready, rstd_ready)

            def node_copies(s, n1, last):
                if not last:
                    act.wait_ge(xnT_done, n1)
                    nc.scalar.copy(xnT[0:D, :], xnT_ps).then_inc(xnT_ready, 1)
                    act.wait_ge(uo_done, n1)
                    nc.scalar.copy(u_out[s][:], uo_ps).then_inc(uo_ready, 1)

            def layer_weights(l, last):
                nc.scalar.copy(ve_cur[:], ve_all[:, bass.ds(l, 1), :].rearrange("p a d -> p (a d)"))
                ins = nc.scalar.copy(vec_cur[:], vec_all[:, bass.ds(l, 1), :].rearrange("p a d -> p (a d)"))
                if not last:
                    ins = nc.scalar.copy(g_next[:], g_all[:, bass.ds(l + 1, 1), :].rearrange("p a d -> p (a d)"))
                ins.then_inc(layer_w, 1)

            def chunk(l, c, s, last, before, more):
                n = act.snap(l * C + c)
                n1 = act.snap(n + 1)
                if before:
                    copy_sums(1 - s % 2, n)
                if more:
                    mask_rows(n + 2)
                act.wait_ge(old_done, n1)
                nc.scalar.copy(old[:], old_ps).then_inc(old_ready, 1)
                if before:
                    copy_aggT(n)
                factor(1, n1)
                if before:
                    node_std(n, c, last)
                exponentials(n1)
                if before:
                    node_copies((s - 1) % SLOTS, n, last)

            def sorted_layer(l, last):
                layer_weights(l, last)
                mask_rows(l * C + 1)
                for s in range(SLOTS):
                    chunk(l, s, s, last, s > 0, True)
                with act.Fori(1, GROUPS - 1) as g:
                    for s in range(SLOTS):
                        chunk(l, g * SLOTS + s, s, last, True, True)
                for s in range(SLOTS):
                    chunk(l, C - SLOTS + s, s, last, True, s < SLOTS - 1)
                n = act.snap(l * C + C)
                copy_sums(1, n)
                copy_aggT(n)
                node_std(n, C, last)
                node_copies(SLOTS - 1, n, last)

            def general_layer(l, last):
                layer_weights(l, last)
                with act.Fori(0, C * NWIN) as j:
                    n1 = act.snap(l * (C * NWIN) + j + 1)
                    mask_rows(n1)
                    factor(W, n1)
                    exponentials(n1)
                    copy_sums(0, n1)
                with act.Fori(0, NWIN) as w:
                    n1 = act.snap(l * NWIN + w + 1)
                    copy_aggT(n1)
                    node_std(n1, w + 1, last)
                    node_copies(0, n1, last)

            act.wait_ge(flag_ready, 1)
            general = act.value_load(flag_i[:], min_val=0, max_val=1)
            with act.If(general):
                with act.Fori(0, L - 1) as l:
                    general_layer(l, False)
                general_layer(L - 1, True)
            with act.Else():
                with act.Fori(0, L - 1) as l:
                    sorted_layer(l, False)
                sorted_layer(L - 1, True)

        @block.vector
        def _(dve):
            nc.vector.memset(ones[:], 1.0)
            nc.vector.memset(eps_t[:], LN_EPS)
            nc.vector.memset(xnT[D:D + 1, :], 1.0)
            nc.vector.memset(xT1[D:D + 1, :], 1.0)
            for s in range(SLOTS):
                nc.vector.memset(feat[s][:, :, F2:UC], 1.0)
            for k in range(2):
                nc.vector.memset(state[k][:, 0:UC], 0.0)
                ins = nc.vector.memset(state[k][:, UC:SC], M_INIT)
            ins.then_inc(const_ready, 1)
            dve.wait_ge(src_loaded, 16)
            for s in range(SLOTS):
                nc.vector.tensor_copy(idx[s][:], src_l[:, s * T:(s + 1) * T]).then_inc(idx_ready, 1)
            for l in range(1, L):
                nc.vector.tensor_scalar(src_l[:, l * C * T:(l + 1) * C * T], src_l[:, 0:C * T], float((l - 1) * NP), None, ALU.add)
            dve.wait_ge(dst_loaded, 16)
            nc.vector.tensor_copy(dst_f[:], dst_i[:]).then_inc(dst_ready, 1)
            dve.wait_ge(iota_ready, 2)
            nc.vector.tensor_copy(iota_n[:], iota_i[:])
            nc.vector.tensor_scalar(wbase[:], iota_i[:, 0:NWIN], float(W), None, ALU.mult)
            nc.vector.tensor_scalar(row_id[:], diag_i[:, 0:1], -1.0, None, ALU.mult)
            nc.vector.tensor_scalar(ident[:], diag_i[:], 0.0, None, ALU.is_equal)
            nc.vector.tensor_scalar(ident_b[:], diag_i[:], 0.0, None, ALU.is_equal).then_inc(const_ready, 1)
            dve.wait_ge(const_ready, 2)
            dve.wait_ge(base_mm, 1)
            nc.vector.tensor_copy(base_b[:], max_ps[:, 0:C + 1]).then_inc(base_ready, 1)
            dve.wait_ge(base_ready, 1)
            nc.vector.memset(step_b[:, 0:1], float(W))
            nc.vector.tensor_tensor(step_b[:, 1:C], base_b[:, 1:C], base_b[:, 0:C - 1], ALU.subtract).then_inc(test_step, 1)
            dve.wait_ge(test_step, 1)
            nc.vector.tensor_scalar(sel_all[:], step_b[0:W + 1, :], row_id[0:W + 1, :], None, ALU.is_equal)
            nc.vector.memset(lim[:, C - 1:C], float(W - 1))
            nc.vector.tensor_scalar(lim[:, 0:C - 1], step_b[:, 1:C], float(W - 1), None, ALU.min).then_inc(test_step, 1)
            full = dst_f[:, 0:C * T].rearrange("p (c t) -> p c t", t=T)
            nc.vector.tensor_tensor(far[:], full, base_b[:, 0:C].unsqueeze(2).to_broadcast([P, C, T]),
                                    ALU.subtract).then_inc(test_step, 1)
            dve.wait_ge(test_step, 3)
            nc.vector.tensor_tensor(wide[:], far[:], lim[:].unsqueeze(2).to_broadcast([P, C, T]), ALU.is_gt).then_inc(test_step, 1)
            dve.wait_ge(test_step, 4)
            nc.vector.scalar_tensor_tensor(wide[:], full, float(PAD_DST), wide[:], ALU.is_lt, ALU.mult).then_inc(test_step, 1)
            dve.wait_ge(test_step, 5)
            nc.vector.scalar_tensor_tensor(wide[:], far[:], 0.0, wide[:], ALU.is_lt, ALU.add).then_inc(test_step, 1)
            dve.wait_ge(test_step, 6)
            nc.vector.tensor_reduce(bad[:, 0:1], wide[:], AX.XY, ALU.add)
            nc.vector.tensor_scalar(lim[:], step_b[:], float(W), None, ALU.is_gt).then_inc(test_step, 1)
            nc.vector.tensor_scalar(bad[:, 2:3], base_b[:, 0:1], 0.0, float(FORCE_GENERAL), ALU.is_gt, ALU.add)
            nc.vector.tensor_scalar(bad[:, 3:4], base_b[:, C - 1:C], float(N - W), None, ALU.is_lt)
            dve.wait_ge(test_step, 7)
            nc.vector.tensor_reduce(bad[:, 1:2], lim[:], AX.X, ALU.add).then_inc(test_step, 1)
            dve.wait_ge(test_step, 8)
            nc.vector.tensor_reduce(bad_n[:], bad[:], AX.X, ALU.add).then_inc(bad_ready, 1)
            dve.wait_ge(bad_mm, 1)
            nc.vector.tensor_scalar(flag_f[:], max_ps[0:1, 256:257], 1.0, None, ALU.min).then_inc(test_step, 1)
            dve.wait_ge(test_step, 9)
            nc.vector.tensor_copy(flag_i[:], flag_f[:]).then_inc(flag_ready, 1)

            def node_mask(c, base, k, n1):
                nc.vector.tensor_scalar(rel[:], dst_f[:, bass.ds(c * T, T)], base, None, ALU.subtract).then_inc(rel_ready, 1)
                dve.wait_ge(rel_ready, n1)
                nc.vector.tensor_tensor(ne[k][:], rel[:].unsqueeze(2).to_broadcast([P, T, W]),
                                        iota_n[:, 0:W].unsqueeze(1).to_broadcast([P, T, W]), ALU.not_equal).then_inc(ne_ready, 1)

            def scores(s, g1, n1):
                dve.wait_ge(u_gathered, n1)
                dve.wait_ge(edge_loaded[s], 16 * g1)
                dve.wait_ge(rows_loaded[s], (16 * T) * g1)
                for t in range(T):
                    ins = nc.vector.tensor_tensor_reduce(dot_out[:, t, :], feat[s][:, t, 0:UC], u_slot(t), 1.0, 0.0,
                                                         ALU.mult, ALU.add, alpha[:, t:t + 1])
                ins.then_inc(dots_done, 1)

            def maxima(k, n1):
                dve.wait_ge(dots_done, n1)
                nc.vector.scalar_tensor_tensor(score[:], ne[k][:], -BIG, alpha[:].unsqueeze(2).to_broadcast([P, T, W]),
                                               ALU.mult, ALU.add).then_inc(score_ready, 1)
                dve.wait_ge(score_ready, n1)
                nc.vector.tensor_reduce(cmax[:], score[:].rearrange("p t n -> p n t"), AX.X, ALU.max).then_inc(cmax_ready, 1)

            def subtract_max(n1):
                dve.wait_ge(m_bc_done, n1)
                nc.vector.tensor_tensor(score[:], score[:], m_bc.unsqueeze(1).to_broadcast([P, T, W]),
                                        ALU.subtract).then_inc(shifted, 1)

            def node_inverse(k, s, n1):
                nc.vector.tensor_scalar(d_pos[:], state[k][0:W, F2:UC], 1e-30, None, ALU.max).then_inc(dpos_ready, 1)
                dve.wait_ge(dpos_ready, n1)
                nc.vector.reciprocal(d_inv[:], d_pos[:]).then_inc(dinv_ready, 1)
                dve.wait_ge(dinv_ready, n1)
                nc.vector.tensor_tensor(some[:], state[k][0:W, F2:UC], d_inv[:], ALU.mult).then_inc(some_ready, 1)
                dve.wait_ge(some_ready, n1)
                nc.vector.scalar_tensor_tensor(skip[:], vec_cur[:, 0:D], some[:], u_win[s][0:W, UC:UW], ALU.mult,
                                               ALU.add).then_inc(skip_ready, 1)

            def node_out(n1, c1, last):
                dve.wait_ge(o_done, n1)
                dve.wait_ge(skip_ready, n1)
                nc.vector.scalar_tensor_tensor(xo[:], o_ps, d_inv[:], skip[:], ALU.mult, ALU.add).then_inc(xo_ready, 1)
                dve.wait_ge(xo_ready, n1)
                nc.vector.tensor_scalar(xr[:], xo[:], 0.0, None, ALU.max).then_inc(xr_ready, 1)
                dve.wait_ge(xr_ready, n1)
                if last:
                    nc.vector.tensor_reduce(mx[:], xr[:], AX.X, ALU.max).then_inc(mx_ready, 1)
                    dve.wait_ge(mx_ready, c1)
                    nc.vector.tensor_scalar(mneg[:], mx[:], -1.0, None, ALU.mult).then_inc(mneg_ready, 1)
                else:
                    nc.vector.bn_stats(bns[:], xr[:]).then_inc(bns_ready, 1)
                    dve.wait_ge(bns_ready, n1)
                    dve.sem_inc(dve_mark, 1)
                    nc.vector.bn_aggr(mv[:], bns[:]).then_inc(mv_ready, 1)

            def node_norm(s, n1, c1, last, x0_here=None):
                if last:
                    dve.wait_ge(lse_ready, c1)
                    nc.vector.tensor_tensor(shift[:], mx[:], lse[:], ALU.add).then_inc(shift_ready, 1)
                    if x0_here is not None:
                        dve.wait_ge(x0_loaded[s], x0_here)
                    dve.wait_ge(shift_ready, c1)
                    nc.vector.scalar_tensor_tensor(xn[:], xr[:], shift[:], x0[s][:], ALU.subtract,
                                                   ALU.add).then_inc(logp_ready, 1)
                    dve.wait_ge(logp_ready, c1)
                    nc.vector.bn_stats(bns[:], xn[:]).then_inc(res_bns, 1)
                    dve.wait_ge(res_bns, c1)
                    dve.sem_inc(dve_mark, 1)
                    nc.vector.bn_aggr(mv[:], bns[:]).then_inc(res_mv, 1)
                    dve.wait_ge(res_rstd, c1)
                    nc.vector.tensor_scalar(xnew[s][:], xn[:], mv[:, 0:1], rstd[:], ALU.subtract, ALU.mult).then_inc(res_ready, 1)
                else:
                    dve.wait_ge(mv_ready, n1)
                    nc.vector.scalar_tensor_tensor(xn[:], xr[:], mv[:, 0:1], vec_cur[:, D:2 * D], ALU.subtract,
                                                   ALU.mult).then_inc(xn_ready, 1)
                    dve.wait_ge(rstd_ready, n1)
                    dve.wait_ge(xn_ready, n1)
                    nc.vector.scalar_tensor_tensor(xnew[s][:], xn[:], rstd[:], vec_cur[:, 2 * D:3 * D], ALU.mult,
                                                   ALU.add).then_inc(xnew_ready, 1)

            def merge(k, n1):
                dve.wait_ge(sums_copied, n1)
                dve.wait_ge(mfac_ready, n1)
                nc.vector.scalar_tensor_tensor(state[k][0:1, 0:UC], old[:, 0:UC], m_fac[0:1, :], state[k][0:1, 0:UC],
                                               ALU.mult, ALU.add).then_inc(merged, 1)

            def chunk(l, c, g1, s, last, before, more, more_idx):
                n = dve.snap(l * C + c)
                n1 = dve.snap(n + 1)
                k = s % 2
                ps = (s - 1) % SLOTS
                scores(s, g1, n1)
                if more_idx:
                    nc.vector.tensor_copy(idx[s][:], src_l[:, bass.ds((n + SLOTS) * T, T)]).then_inc(idx_ready, 1)
                if before:
                    dve.wait_ge(prob_ready, n)
                maxima(k, n1)
                if more:
                    node_mask(c + 1, base_b[:, bass.ds(c + 1, 1)], 1 - k, n + 2)
                if before:
                    merge(1 - k, n)
                nc.vector.tensor_copy(sel[:], sel_all[:, bass.ds(c, 1)]).then_inc(sel_ready, 1)
                dve.wait_ge(cmT_done, n1)
                nc.vector.tensor_reduce(cm[:], cmT, AX.X, ALU.max).then_inc(cm_ready, 1)
                if before:
                    dve.wait_ge(merged, n)
                    node_inverse(1 - k, ps, n)
                dve.wait_ge(cm_ready, n1)
                dve.wait_ge(old_ready, n1)
                nc.vector.tensor_tensor(cm[0:1, :], cm[0:1, :], old[:, UC:SC], ALU.max).then_inc(m_ready, 1)
                dve.wait_ge(m_ready, n1)
                nc.vector.tensor_scalar(diag[:], ident[0:W, 0:W], cm[:], M_INIT, ALU.mult, ALU.max).then_inc(diag_ready, 1)
                nc.vector.tensor_tensor(m_dif[0:1, :], old[:, UC:SC], cm[0:1, :], ALU.subtract).then_inc(mdif_ready, 1)
                nc.vector.tensor_scalar(state[k][0:W, UC:SC], cm[:], M_INIT, None, ALU.max)
                if before:
                    node_out(n, c, last)
                subtract_max(n1)
                if before:
                    node_norm(ps, n, c, last, 16 * (g1 - (L - 1) * GROUPS - (s == 0)) if last else None)

            def sorted_layer(l, last):
                n0 = dve.snap(l * C)
                dve.wait_ge(layer_w, l + 1)
                node_mask(0, base_b[:, 0:1], 0, n0 + 1)
                for s in range(SLOTS):
                    chunk(l, s, l * GROUPS + 1, s, last, s > 0, True, True)
                with dve.Fori(1, GROUPS - 1) as g:
                    g1 = dve.snap(l * GROUPS + g + 1)
                    for s in range(SLOTS):
                        chunk(l, g * SLOTS + s, g1, s, last, True, True, True)
                for s in range(SLOTS):
                    chunk(l, C - SLOTS + s, l * GROUPS + GROUPS, s, last, True, s < SLOTS - 1, not last)
                n = dve.snap(l * C + C)
                merge(1, n)
                dve.wait_ge(merged, n)
                node_inverse(1, SLOTS - 1, n)
                node_out(n, C, last)
                node_norm(SLOTS - 1, n, C, last, 16 * GROUPS if last else None)

            def general_step(l, c, g1, s, w):
                n1 = dve.snap(l * (C * NWIN) + c * NWIN + w + 1)
                m_old = all_flat[:, bass.ds(w * SC + UC, 1)]
                sums = all_flat[:, bass.ds(w * SC, UC)]
                node_mask(c, wbase[:, bass.ds(w, 1)], 0, n1)
                scores(s, g1, n1)
                maxima(0, n1)
                dve.wait_ge(cmT_done, n1)
                nc.vector.tensor_reduce(cm[:], cmT, AX.X, ALU.max).then_inc(cm_ready, 1)
                dve.wait_ge(cm_ready, n1)
                nc.vector.tensor_tensor(m_new[:], cm[:], m_old, ALU.max).then_inc(m_ready, 1)
                dve.wait_ge(m_ready, n1)
                nc.vector.tensor_scalar(diag[:], ident[0:W, 0:W], m_new[:], None, ALU.mult).then_inc(diag_ready, 1)
                nc.vector.tensor_tensor(m_dif[:], m_old, m_new[:], ALU.subtract).then_inc(mdif_ready, 1)
                subtract_max(n1)
                dve.wait_ge(sums_copied, n1)
                dve.wait_ge(mfac_ready, n1)
                nc.vector.scalar_tensor_tensor(sums, sums, m_fac[:], state[0][0:W, 0:UC], ALU.mult, ALU.add)
                nc.vector.tensor_copy(m_old, m_new[:]).then_inc(window_merged, 1)
                dve.wait_ge(window_merged, n1)

            def general_layer(l, last):
                dve.wait_ge(layer_w, l + 1)
                nc.vector.memset(all_flat, 0.0).then_inc(state_set, 1)
                dve.wait_ge(state_set, 2 * l + 1)
                nc.vector.memset(all_state[:, :, UC:SC], M_INIT).then_inc(state_set, 1)
                dve.wait_ge(state_set, 2 * l + 2)
                dve.sem_inc(dve_mark, 1)
                with dve.Fori(0, GROUPS) as g:
                    g1 = dve.snap(l * GROUPS + g + 1)
                    for s in range(SLOTS):
                        c = dve.snap(g * SLOTS + s)
                        with dve.Fori(0, NWIN) as w:
                            general_step(l, c, g1, s, w)
                        nc.vector.memset(m_dif[:], 0.0).then_inc(merged, 1)
                        dve.wait_ge(merged, l * C + c + 1)
                        nxt = dve.snap((l * C + c + SLOTS) * T)
                        if last:
                            nxt = dve.snap(c * T)
                        nc.vector.tensor_copy(idx[s][:], src_l[:, bass.ds(nxt, T)]).then_inc(idx_ready, 1)
                with dve.Fori(0, NWIN) as w:
                    n1 = dve.snap(l * NWIN + w + 1)
                    nc.vector.tensor_copy(state[0][0:W, :], all_flat[:, bass.ds(w * SC, SC)]).then_inc(state_got, 1)
                    dve.wait_ge(state_got, n1)
                    dve.wait_ge(win_loaded, l * STEPS + C * NWIN + w + 1)
                    node_inverse(0, 0, n1)
                    node_out(n1, w + 1, last)
                    node_norm(0, n1, w + 1, last)
                    dve.wait_ge(rows_kept, n1)

            dve.wait_ge(flag_ready, 1)
            general = dve.value_load(flag_i[:], min_val=0, max_val=1)
            with dve.If(general):
                dve.wait_ge(u_stored, 16 * U0N)
                with dve.Fori(0, L - 1) as l:
                    general_layer(l, False)
                general_layer(L - 1, True)
            with dve.Else():
                with dve.Fori(0, L - 1) as l:
                    sorted_layer(l, False)
                sorted_layer(L - 1, True)

        @block.tensor
        def _(pe):
            pe.sem_inc(win_free, 1)
            pe.wait_ge(const_ready, 1)
            pe.wait_ge(dst_ready, 1)
            firsts = dst_f[0:1, :].rearrange("p (c t) -> p c t", t=T)[:, :, 0]
            nc.tensor.matmul(max_ps[:, 0:C + 1], ones[0:1, :], firsts, start=True, stop=True).then_inc(base_mm, 1)
            pe.wait_ge(weights_loaded, 16 * N_WEIGHTS)
            for l in range(L):
                nc.tensor.matmul(u_ps[0:D + 1, l, 0:UC], qT_sb[:, l, :], ke_sb[:, l, :], start=True, stop=True).then_inc(g_mm, 1)
            pe.wait_ge(g_ready, L)
            for i in range(U0N):
                if i >= 2:
                    pe.wait_ge(u0_copied, i - 1)
                for b in range(U0B):
                    r = (i * U0B + b) * P
                    ins = nc.tensor.matmul(u_ps[:, 2 * (i % 2) + b // 2, (b % 2) * 256:(b % 2) * 256 + UW], xT1[:, r:r + P],
                                           g_all[:, 0, :], start=True, stop=True)
                ins.then_inc(u0_mm, 1)
            pe.wait_ge(bad_ready, 1)
            pe.wait_ge(base_ready, 1)
            nc.tensor.matmul(max_ps[0:1, 256:257], bad_n[:], ones[:, 0:1], start=True, stop=True).then_inc(bad_mm, 1)

            def turn_mask(k, n1):
                pe.wait_ge(ne_ready, n1)
                for t in range(0, T, 2):
                    w = min(2, T - t) * W
                    ins = nc.tensor.transpose(neT_ps[0:w, t // 2, :], ne[k][:, t:t + w // W, :].rearrange("p t n -> p (t n)"),
                                              ident_b[:])
                ins.then_inc(neT_done, 1)

            def gather_u(s, n1):
                pe.wait_ge(mT_ready, n1)
                for t in range(T):
                    h = slice((t % 2) * W, (t % 2) * W + W)
                    ins = nc.tensor.matmul(u_slot(t), mT[h, t // 2, :], u_win[s][h, 0:UC], start=True, stop=True)
                ins.then_inc(u_gathered, 1)

            def turn_max(n1):
                pe.wait_ge(cmax_ready, n1)
                pe.sem_inc(pe_mark, 1)
                nc.tensor.transpose(cmT, cmax[:], ident[:]).then_inc(cmT_done, 1)

            def spread_max(n1):
                pe.wait_ge(diag_ready, n1)
                nc.tensor.matmul(m_bc, ones[0:W, :], diag[:], start=True, stop=True).then_inc(m_bc_done, 1)

            def sums(s, n1):
                pe.wait_ge(prob_ready, n1)
                for t in range(T):
                    ins = nc.tensor.matmul(agg, prob[:, t, :], feat[s][:, t, 0:UC], start=(t == 0), stop=(t == T - 1))
                ins.then_inc(agg_done, 1)

            def turn_sums(k):
                nc.tensor.transpose(aggT_ps, state[k][0:W, 0:F2], ident[0:W, 0:W]).then_inc(aggT_done, 1)

            def node_product(n1):
                pe.wait_ge(aggT_ready, n1)
                nc.tensor.matmul(o_ps, aggT[:], ve_cur[:], start=True, stop=True).then_inc(o_done, 1)

            def node_rows(s, n1):
                pe.wait_ge(xnew_ready, n1)
                pe.sem_inc(pe_mark, 1)
                nc.tensor.transpose(xnT_ps, xnew[s][:], ident[0:W, 0:W]).then_inc(xnT_done, 1)
                pe.wait_ge(xnT_ready, n1)
                nc.tensor.matmul(uo_ps, xnT[:], g_next[:], start=True, stop=True).then_inc(uo_done, 1)

            def chunk(l, c, g1, s, last, before, more):
                n = pe.snap(l * C + c)
                n1 = pe.snap(n + 1)
                k = s % 2
                turn_max(n1)
                if more:
                    turn_mask(1 - k, n + 2)
                if before:
                    pe.wait_ge(merged, n)
                    pe.sem_inc(pe_mark, 1)
                    turn_sums(1 - k)
                pe.wait_ge(sel_ready, n1)
                pe.sem_inc(pe_mark, 1)
                nc.tensor.matmul(old_ps, sel[:], state[1 - k][:], start=True, stop=True).then_inc(old_done, 1)
                spread_max(n1)
                if before:
                    node_product(n)
                if more:
                    pe.wait_ge(uwin_loaded[(s + 1) % SLOTS], 32 * (g1 + 1 if s == SLOTS - 1 else g1))
                    gather_u((s + 1) % SLOTS, n + 2)
                sums(s, n1)
                if before and not last:
                    node_rows((s - 1) % SLOTS, n)
                    pe.wait_ge(uo_ready, n)
                    pe.sem_inc(pe_mark, 1)

            def sorted_layer(l, last):
                pe.wait_ge(layer_w, l + 1)
                turn_mask(0, l * C + 1)
                pe.wait_ge(uwin_loaded[0], 32 * (l * GROUPS + 1))
                gather_u(0, l * C + 1)
                for s in range(SLOTS):
                    chunk(l, s, l * GROUPS + 1, s, last, s > 0, True)
                with pe.Fori(1, GROUPS - 1) as g:
                    g1 = pe.snap(l * GROUPS + g + 1)
                    for s in range(SLOTS):
                        chunk(l, g * SLOTS + s, g1, s, last, True, True)
                for s in range(SLOTS):
                    chunk(l, C - SLOTS + s, l * GROUPS + GROUPS, s, last, True, s < SLOTS - 1)
                n = pe.snap(l * C + C)
                pe.wait_ge(merged, n)
                pe.sem_inc(pe_mark, 1)
                turn_sums(1)
                node_product(n)
                if not last:
                    node_rows(SLOTS - 1, n)
                    pe.wait_ge(uo_ready, n)

            def general_layer(l, last):
                pe.wait_ge(layer_w, l + 1)
                pe.sem_inc(pe_mark, 1)
                with pe.Fori(0, GROUPS) as g:
                    for s in range(SLOTS):
                        with pe.Fori(0, NWIN) as w:
                            j = pe.snap((g * SLOTS + s) * NWIN + w)
                            n1 = pe.snap(l * (C * NWIN) + j + 1)
                            turn_mask(0, n1)
                            pe.wait_ge(win_loaded, l * STEPS + j + 1)
                            gather_u(0, n1)
                            turn_max(n1)
                            spread_max(n1)
                            sums(s, n1)
                            pe.wait_ge(window_merged, n1)
                            pe.sem_inc(win_free, 1)
                with pe.Fori(0, NWIN) as w:
                    n1 = pe.snap(l * NWIN + w + 1)
                    pe.wait_ge(state_got, n1)
                    pe.sem_inc(pe_mark, 1)
                    turn_sums(0)
                    node_product(n1)
                    if not last:
                        node_rows(0, n1)
                        pe.wait_ge(uo_ready, n1)
                    pe.wait_ge(rows_kept, n1)
                    pe.sem_inc(win_free, 1)

            pe.wait_ge(flag_ready, 1)
            general = pe.value_load(flag_i[:], min_val=0, max_val=1)
            with pe.If(general):
                with pe.Fori(0, L - 1) as l:
                    general_layer(l, False)
                general_layer(L - 1, True)
            with pe.Else():
                with pe.Fori(0, L - 1) as l:
                    sorted_layer(l, False)
                sorted_layer(L - 1, True)


def kernel(**inputs):
    import numpy as np
    import concourse.bacc as bacc
    from concourse.bass_utils import run_bass_kernel_spmd

    a = {k.replace("L0_gnn_", ""): np.asarray(v) for k, v in inputs.items()}

    def chunked(edges, fill):
        full = np.concatenate([edges, np.full(C * EC - E, fill, edges.dtype)])
        return full.reshape(C, P, T).transpose(1, 0, 2)

    x_rows = np.concatenate([a["x"], np.zeros((NP - N, D), a["x"].dtype)])
    dst = chunked(a["dst"], PAD_DST)
    ea = a["edge_attr_64"]
    none = np.zeros((1, D), a["ln_gamma"].dtype)
    vec = np.concatenate([a["bv"], np.concatenate([a["ln_gamma"], none]), np.concatenate([a["ln_beta"], none])], 1)
    arrays = {
        "x": x_rows,
        "xT": x_rows.T,
        "src": chunked(a["src"], 0).reshape(P, C * T),
        "dst": np.concatenate([dst, dst[:, 0:1]], 1).reshape(P, (C + 1) * T),
        "edge": np.concatenate([ea, np.zeros((C * EC - E, D), ea.dtype)]).reshape(C, P, T * D),
        "w_qT": np.concatenate([a["Wq"], a["bq"][:, None, :]], 1).transpose(2, 0, 1),
        "w_ke": np.concatenate([a["Wk"].transpose(0, 2, 1), a["We"].transpose(0, 2, 1), a["bk"][:, :, None]], 2).transpose(1, 0, 2),
        "w_sk": np.concatenate([a["Ws"], a["bs"][:, None, :]], 1).transpose(1, 0, 2),
        "w_ve": np.concatenate([a["Wv"], a["We"]], 1).transpose(1, 0, 2),
        "w_vec": np.broadcast_to(vec[None], (W, L, 3 * D)),
    }
    arrays = {k: np.ascontiguousarray(v) for k, v in arrays.items()}
    nc = bacc.Bacc("TRN2", target_bir_lowering=False, num_devices=1)
    aps = {k: nc.dram_tensor(k, v.shape, mybir.dt.from_np(v.dtype), kind="ExternalInput").ap() for k, v in arrays.items()}
    aps["out"] = nc.dram_tensor("out", (NP, D), F32, kind="ExternalOutput").ap()
    aps["x_table"] = nc.dram_tensor("x_table", ((L - 1) * NP, D), F32, kind="Internal").ap()
    aps["u_table"] = nc.dram_tensor("u_table", (L * NP, UW), F32, kind="Internal").ap()
    gnn_kernel(nc, **aps)
    r = run_bass_kernel_spmd(nc, [arrays], core_ids=[0])
    return r.results[0]["out"][:N]
```

```python
from contextlib import ExitStack

import concourse.bass as bass
from concourse import mybir

F32 = mybir.dt.float32
BF16 = mybir.dt.bfloat16
I32 = mybir.dt.int32
ALU = mybir.AluOpType
ACT = mybir.ActivationFunctionType
AX = mybir.AxisListType

N, E, D, L = 6250, 206250, 64, 3
P = 128
T = 13
T_FIRST = 9
EC = T * P
SLOTS = 4
GROUPS = -(-E // (EC * SLOTS))
C = GROUPS * SLOTS
W = 64
NWIN = -(-N // W)
U0B = 4
U0N = -(-(N + W) // (U0B * P))
NP = U0N * U0B * P
PAD_DST = 1 << 20
F2 = 2 * D
UC = F2 + 1
FP = 3 * D
UW = UC + D
SC = UC + 1
UPITCH = 160
BIG = 3.0e38
M_INIT = -1.5e38
LN_EPS = 1e-5
U0_FIRST = min(4, U0N)
FORCE_GENERAL = 0
assert SLOTS * W <= U0_FIRST * U0B * P


def gnn_kernel(nc, x, xT, src, dst, edge, w_qT, w_ke, w_sk, w_ve, w_vec, out, x_table, u_table):
    with ExitStack() as ctx:
        def sb(name, shape, dt=F32):
            return ctx.enter_context(nc.sbuf_tensor(name, shape, dt))

        def ps(name, shape, dt=F32):
            return ctx.enter_context(nc.psum_tensor(name, shape, dt))

        def sem(name):
            return ctx.enter_context(nc.semaphore(name))

        dst_i = sb("dst_i", [P, (C + 1) * T], I32)
        dst_f = sb("dst_f", [P, (C + 1) * T])
        src_l = sb("src_l", [P, (L * C + SLOTS) * T], I32)
        base_b = sb("base_b", [P, C + 1])
        step_b = sb("step_b", [P, C])
        wbase = sb("wbase", [P, NWIN])
        sel_all = sb("sel_all", [W + 1, C])
        diag_i = sb("diag_i", [P, P], I32)
        iota_i = sb("iota_i", [P, P], I32)
        ident = sb("ident", [P, P])
        ident_b = sb("ident_b", [P, P], BF16)
        row_id = sb("row_id", [P, 1])
        ones = sb("ones", [P, P])
        eps_t = sb("eps_t", [P, 1])
        xT1 = sb("xT1", [D + 1, NP])
        qT_sb = sb("qT_sb", [D, L, D + 1])
        ke_sb = sb("ke_sb", [D, L, UC])
        g_all = sb("g_all", [D + 1, L, UW])
        ve_all = sb("ve_all", [F2, L, D])
        vec_all = sb("vec_all", [W, L, 3 * D])
        far = sb("far", [P, C, T])
        wide = sb("wide", [P, C, T])
        lim = sb("lim", [P, C])
        bad = sb("bad", [P, 4])
        bad_n = sb("bad_n", [P, 1])
        flag_f = sb("flag_f", [1, 1])
        flag_i = sb("flag_i", [1, 1], I32)
        g_next = sb("g_next", [D + 1, UW])
        ve_cur = sb("ve_cur", [F2, D])
        vec_cur = sb("vec_cur", [W, 3 * D])
        feat = [sb(f"feat{s}", [P, T, FP]) for s in range(SLOTS)]
        idx = [sb(f"idx{s}", [P, T], I32) for s in range(SLOTS)]
        u_win = [sb(f"u_win{s}", [P, UW]) for s in range(SLOTS)]
        x0 = [sb(f"x0{s}", [W, D]) for s in range(SLOTS)]
        xnew = [sb(f"xnew{s}", [W, D]) for s in range(SLOTS)]
        u_out = [sb(f"u_out{s}", [W, UW]) for s in range(SLOTS)]
        rel = [sb(f"rel{k}", [P, T]) for k in range(2)]
        ne = [sb(f"ne{k}", [P, T, W], BF16) for k in range(2)]
        mT = sb("mT", [P, T + 1, P], BF16)
        mT_by = mT[:].rearrange("p (j two) e -> p two j e", two=2)
        u_parts = sb("u_parts", [P, 2 * UC], BF16)
        u_rest = sb("u_rest", [P, UC])
        u_mid = sb("u_mid", [W, UC], BF16)
        dot_out = sb("dot_out", [P, T, UC], BF16)
        alpha = sb("alpha", [P, T])
        score = sb("score", [P, T, W])
        prob = sb("prob", [P, T, W])
        cmax = sb("cmax", [P, W])
        cm = sb("cm", [W, 1])
        m_new = sb("m_new", [W, 1])
        diag = sb("diag", [W, W])
        sel = sb("sel", [W + 1, 1])
        old = sb("old", [1, SC])
        m_dif = sb("m_dif", [W, 1])
        m_fac = sb("m_fac", [W, 1])
        state = [sb(f"state{k}", [W + 1, SC]) for k in range(2)]
        d_pos = sb("d_pos", [W, 1])
        d_inv = sb("d_inv", [W, 1])
        some = sb("some", [W, 1])
        skip = sb("skip", [W, D])
        aggT = sb("aggT", [F2, W])
        xo = sb("xo", [W, D])
        xr = sb("xr", [W, D])
        bns = sb("bns", [W, 6])
        mv = sb("mv", [W, 2])
        lnv = sb("lnv", [W, 1])
        rstd = sb("rstd", [W, 1])
        xn = sb("xn", [W, D])
        xnT = sb("xnT", [D + 1, W])
        mx = sb("mx", [W, 1])
        mneg = sb("mneg", [W, 1])
        ex = sb("ex", [W, D])
        esum = sb("esum", [W, 1])
        lse = sb("lse", [W, 1])
        shift = sb("shift", [W, 1])
        big = sb("big", [P, max(U0N * U0B * UW, NWIN * SC)])
        u0_out = big[:, 0:U0N * U0B * UW].rearrange("p (b f) -> p b f", f=UW)
        all_flat = big[0:W, 0:NWIN * SC]
        all_state = all_flat.rearrange("p (w f) -> p w f", f=SC)

        u_ps = ps("u_ps", [P, 6, 512])
        neT_ps = u_ps[:, 5, :].bitcast(BF16).rearrange("p (j e) -> p j e", e=P)
        iota_w = u_ps[:, 5, 512 - W:]
        max_ps = ps("max_ps", [P, 512])
        agg_ps = ps("agg_ps", [P, 512])
        cmT = max_ps[0:W, 0:P]
        m_bc = max_ps[:, P:P + W]
        xnT_ps = max_ps[0:D, P + W:P + 2 * W]
        uo_ps = max_ps[0:W, 2 * P:2 * P + UW]
        agg = agg_ps[0:W, 0:UC]
        o_ps = agg_ps[0:W, 136:136 + D]
        aggT_ps = agg_ps[:, 200:200 + W]
        old_ps = agg_ps[0:1, 264:264 + SC]

        def u_slot(t):
            return u_ps[:, t // 3, (t % 3) * UPITCH:(t % 3) * UPITCH + UC]

        src_loaded = sem("src_loaded")
        dst_loaded = sem("dst_loaded")
        weights_loaded = sem("weights_loaded")
        x_filled = sem("x_filled")
        iota_ready = sem("iota_ready")
        const_ready = sem("const_ready")
        dst_ready = sem("dst_ready")
        base_mm = sem("base_mm")
        base_ready = sem("base_ready")
        test_step = sem("test_step")
        bad_ready = sem("bad_ready")
        bad_mm = sem("bad_mm")
        flag_ready = sem("flag_ready")
        g_mm = sem("g_mm")
        g_ready = sem("g_ready")
        u0_mm = sem("u0_mm")
        u0_copied = sem("u0_copied")
        x_stored = sem("x_stored")
        u_stored = sem("u_stored")
        out_stored = sem("out_stored")
        layer_stored = sem("layer_stored")
        layer_w = sem("layer_w")
        edge_loaded = [sem(f"edge_loaded{s}") for s in range(SLOTS)]
        rows_loaded = [sem(f"rows_loaded{s}") for s in range(SLOTS)]
        rest_loaded = [sem(f"rest_loaded{s}") for s in range(SLOTS)]
        uwin_loaded = [sem(f"uwin_loaded{s}") for s in range(SLOTS)]
        x0_loaded = [sem(f"x0_loaded{s}") for s in range(SLOTS)]
        idx_ready = sem("idx_ready")
        rel_ready = sem("rel_ready")
        ne_ready = sem("ne_ready")
        neT_done = sem("neT_done")
        mT_ready = sem("mT_ready")
        high_ready = sem("high_ready")
        rest_ready = sem("rest_ready")
        mid_ready = sem("mid_ready")
        parts_ready = sem("parts_ready")
        u_gathered = sem("u_gathered")
        dots_done = sem("dots_done")
        score_ready = sem("score_ready")
        cmax_ready = sem("cmax_ready")
        cmT_done = sem("cmT_done")
        cm_ready = sem("cm_ready")
        sel_ready = sem("sel_ready")
        old_done = sem("old_done")
        old_ready = sem("old_ready")
        m_ready = sem("m_ready")
        mdif_ready = sem("mdif_ready")
        mfac_ready = sem("mfac_ready")
        diag_ready = sem("diag_ready")
        m_bc_done = sem("m_bc_done")
        shifted = sem("shifted")
        prob_ready = sem("prob_ready")
        agg_done = sem("agg_done")
        sums_copied = sem("sums_copied")
        merged = sem("merged")
        aggT_done = sem("aggT_done")
        aggT_ready = sem("aggT_ready")
        dpos_ready = sem("dpos_ready")
        dinv_ready = sem("dinv_ready")
        some_ready = sem("some_ready")
        skip_ready = sem("skip_ready")
        o_done = sem("o_done")
        xo_ready = sem("xo_ready")
        xr_ready = sem("xr_ready")
        bns_ready = sem("bns_ready")
        mv_ready = sem("mv_ready")
        lnv_ready = sem("lnv_ready")
        rstd_ready = sem("rstd_ready")
        xn_ready = sem("xn_ready")
        xnew_ready = sem("xnew_ready")
        xnT_done = sem("xnT_done")
        xnT_ready = sem("xnT_ready")
        uo_done = sem("uo_done")
        uo_ready = sem("uo_ready")
        mx_ready = sem("mx_ready")
        mneg_ready = sem("mneg_ready")
        ex_ready = sem("ex_ready")
        lse_ready = sem("lse_ready")
        shift_ready = sem("shift_ready")
        logp_ready = sem("logp_ready")
        res_bns = sem("res_bns")
        res_mv = sem("res_mv")
        res_lnv = sem("res_lnv")
        res_rstd = sem("res_rstd")
        res_ready = sem("res_ready")
        sp_mark = sem("sp_mark")
        pool_mark = sem("pool_mark")
        act_mark = sem("act_mark")
        pe_mark = sem("pe_mark")
        dve_mark = sem("dve_mark")
        win_free = sem("win_free")
        win_landed = sem("win_landed")
        win_loaded = sem("win_loaded")
        rows_stored = sem("rows_stored")
        rows_kept = sem("rows_kept")
        window_merged = sem("window_merged")
        state_set = sem("state_set")
        state_got = sem("state_got")

        N_WEIGHTS = 6
        STEPS = C * NWIN + NWIN
        block = ctx.enter_context(nc.Block())

        def rows(table, row):
            return table[bass.ds(row, W), :]

        @block.sync
        def _(sp):
            sp.dma_start(src_l[:, 0:C * T], src).then_inc(src_loaded, 16)
            sp.dma_start(dst_i[:], dst).then_inc(dst_loaded, 16)
            sp.dma_start(qT_sb[:], w_qT).then_inc(weights_loaded, 16)
            sp.dma_start(ke_sb[:], w_ke).then_inc(weights_loaded, 16)
            sp.dma_start(g_all[:, :, UC:UW], w_sk).then_inc(weights_loaded, 16)
            sp.dma_start(xT1[0:D, :], xT).then_inc(weights_loaded, 16)
            sp.dma_start(ve_all[:], w_ve).then_inc(weights_loaded, 16)
            sp.dma_start(vec_all[:], w_vec).then_inc(weights_loaded, 16)

            def load_edges(c, s):
                e = edge[bass.ds(c, 1), :, :].rearrange("a p (t d) -> (a p) t d", d=D)
                sp.dma_start(feat[s][:, :, D:F2], e).then_inc(edge_loaded[s], 16)

            def load(l, c, s, first):
                node = sp.value_load(dst_i[0:1, bass.ds(c * T, 1)], min_val=0, max_val=N - 1)
                u_row = sp.snap(l * NP + node)
                if not first:
                    free = sp.snap((l * C + c) - (SLOTS - 1))
                    sp.wait_ge(merged, free)
                    sp.sem_inc(sp_mark, 1)
                    sp.wait_ge(skip_ready, free)
                    sp.sem_inc(sp_mark, 1)
                for h in range(2):
                    sp.dma_start(u_win[s][h * W:(h + 1) * W, :], rows(u_table, u_row)).then_inc(uwin_loaded[s], 16)
                load_edges(c, s)

            def load_x(c, s):
                node = sp.value_load(dst_i[0:1, bass.ds(c * T, 1)], min_val=0, max_val=N - 1)
                sp.dma_start(x0[s][:], rows(x, node)).then_inc(x0_loaded[s], 16)

            def store(l, c, s, last, ending=False):
                node = sp.value_load(dst_i[0:1, bass.ds(c * T, 1)], min_val=0, max_val=N - 1)
                if last:
                    c1 = sp.snap(c + 1)
                    sp.wait_ge(res_ready, c1)
                    sp.dma_start(rows(out, node), xnew[s][:]).then_inc(out_stored, 16)
                    sp.wait_ge(out_stored, 16 * c1)
                else:
                    n = sp.snap(l * C + c)
                    x_row = sp.snap(l * NP + node)
                    u_row = sp.snap((l + 1) * NP + node)
                    sp.wait_ge(xnew_ready, n + 1)
                    sp.dma_start(rows(x_table, x_row), xnew[s][:]).then_inc(x_stored, 16)
                    sp.wait_ge(uo_ready, n + 1)
                    sp.dma_start(rows(u_table, u_row), u_out[s][:]).then_inc(u_stored, 16)
                    sp.wait_ge(x_stored, 16 * (n + 1))
                    sp.sem_inc(sp_mark, 1)
                    if ending:
                        sp.sem_inc(layer_stored, 1)
                    sp.wait_ge(u_stored, 16 * (n + 1 + U0N))
                sp.sem_inc(sp_mark, 1)

            def first_loads(l):
                for s in range(SLOTS):
                    load(l, s, s, True)

            def sorted_layer(l, last):
                with sp.Fori(1, GROUPS) as g:
                    for s in range(SLOTS):
                        load(l, g * SLOTS + s, s, False)
                        store(l, (g - 1) * SLOTS + s, s, last)
                        if last:
                            load_x(g * SLOTS + s, s)
                for s in range(SLOTS):
                    store(l, C - SLOTS + s, s, last, s == SLOTS - 1)

            def load_window(row, j):
                sp.wait_ge(win_free, j + 1)
                sp.sem_inc(sp_mark, 1)
                for h in range(2):
                    sp.dma_start(u_win[0][h * W:(h + 1) * W, :], rows(u_table, row)).then_inc(win_landed, 16)
                sp.wait_ge(win_landed, 32)
                sp.sem_clear(win_landed)
                sp.sem_inc(win_loaded, 1)

            def general_layer(l, last):
                with sp.Fori(0, GROUPS) as g:
                    for s in range(SLOTS):
                        c = sp.snap(g * SLOTS + s)
                        load_edges(c, s)
                        with sp.Fori(0, NWIN) as w:
                            load_window(l * NP + w * W, l * STEPS + c * NWIN + w)
                with sp.Fori(0, NWIN) as w:
                    n = sp.snap(l * NWIN + w)
                    row = sp.snap(w * W)
                    if last:
                        sp.dma_start(x0[0][:], rows(x, row)).then_inc(rows_stored, 16)
                        sp.wait_ge(rows_stored, 16)
                        sp.sem_clear(rows_stored)
                    load_window(l * NP + row, l * STEPS + C * NWIN + w)
                    if last:
                        sp.wait_ge(res_ready, w + 1)
                        sp.dma_start(rows(out, row), xnew[0][:]).then_inc(rows_stored, 16)
                        sp.wait_ge(rows_stored, 16)
                    else:
                        x_row = sp.snap(l * NP + row)
                        u_row = sp.snap((l + 1) * NP + row)
                        sp.wait_ge(uo_ready, n + 1)
                        sp.dma_start(rows(x_table, x_row), xnew[0][:]).then_inc(rows_stored, 16)
                        sp.dma_start(rows(u_table, u_row), u_out[0][:]).then_inc(rows_stored, 16)
                        sp.wait_ge(rows_stored, 32)
                    sp.sem_clear(rows_stored)
                    sp.sem_inc(rows_kept, 1)
                sp.sem_inc(layer_stored, 1)

            def store_u0(steps):
                for i in steps:
                    sp.wait_ge(u0_copied, i + 1)
                    r = u_table[i * U0B * P:(i + 1) * U0B * P, :].rearrange("(b p) f -> p b f", p=P)
                    sp.dma_start(r, u0_out[:, i * U0B:(i + 1) * U0B, :]).then_inc(u_stored, 16)

            for l in range(L - 1):
                sp.dma_start(x_table[l * NP:(l + 1) * NP, :], x).then_inc(x_filled, 16)
            store_u0(range(U0_FIRST))
            sp.wait_ge(flag_ready, 1)
            general = sp.value_load(flag_i[:], min_val=0, max_val=1)
            with sp.If(general):
                store_u0(range(U0_FIRST, U0N))
                sp.wait_ge(u_stored, 16 * U0N)
                sp.wait_ge(x_filled, 16 * (L - 1))
                with sp.Fori(0, L - 1) as l:
                    general_layer(l, False)
                general_layer(L - 1, True)
            with sp.Else():
                sp.wait_ge(u_stored, 16 * U0_FIRST)
                first_loads(0)
                store_u0(range(U0_FIRST, U0N))
                sp.wait_ge(u_stored, 16 * U0N)
                sp.wait_ge(x_filled, 16 * (L - 1))
                with sp.Fori(0, L - 1) as l:
                    sorted_layer(l, False)
                    first_loads(l + 1)
                for s in range(SLOTS):
                    load_x(s, s)
                sorted_layer(L - 1, True)
                sp.wait_ge(out_stored, 16 * C)
                sp.wait_ge(x_stored, 16 * (L - 1) * C)
                sp.wait_ge(u_stored, 16 * ((L - 1) * C + U0N))

        @block.gpsimd
        def _(pool):
            nc.gpsimd.iota(iota_i[:], pattern=[[1, P]], base=0, channel_multiplier=0).then_inc(iota_ready, 1)
            nc.gpsimd.iota(diag_i[:], pattern=[[1, P]], base=0, channel_multiplier=-1).then_inc(iota_ready, 1)

            def gather(table, n1, s):
                pool.wait_ge(idx_ready, n1)
                pool.sem_inc(pool_mark, 1)
                for t in range(T):
                    nc.gpsimd.indirect_dma_start(
                        feat[s][:, t, 0:D], None, table, bass.IndirectOffsetOnAxis(idx[s][:, t:t + 1], 0),
                    ).then_inc(rows_loaded[s] if t < T_FIRST else rest_loaded[s], 16)

            def layer(table, l):
                for s in range(SLOTS):
                    gather(table, l * C + s + 1, s)
                with pool.Fori(1, GROUPS) as g:
                    for s in range(SLOTS):
                        n1 = pool.snap((l * C + s + 1) + g * SLOTS)
                        pool.wait_ge(merged, n1 - SLOTS)
                        gather(table, n1, s)

            layer(x, 0)
            with pool.Fori(1, L) as l:
                pool.wait_ge(layer_stored, l)
                layer(x_table, l)

        @block.scalar
        def _(act):
            nc.scalar.preload_act_table_set("natural_log_exp_and_others")
            for l in range(L):
                act.wait_ge(g_mm, l + 1)
                act.wait_ge(weights_loaded, 16 * N_WEIGHTS)
                nc.scalar.activation(g_all[:, l, 0:UC], u_ps[0:D + 1, l, 0:UC], ACT.Copy, scale=D ** -0.5).then_inc(g_ready, 1)
            for i in range(U0N):
                act.wait_ge(u0_mm, i + 1)
                for h in range(2):
                    u2 = u_ps[:, 2 * (i % 2) + h, :].rearrange("p (b f) -> p b f", b=2)[:, :, 0:UW]
                    ins = nc.scalar.copy(u0_out[:, i * U0B + 2 * h:i * U0B + 2 * h + 2, :], u2)
                ins.then_inc(u0_copied, 1)

            def mask_rows(n1):
                act.wait_ge(neT_done, n1)
                for half in (slice(0, W), slice(W, P)):
                    nc.scalar.activation(mT_by[half, 0, 0:(T + 1) // 2, :], neT_ps[0:W, 0:(T + 1) // 2, :], ACT.Copy,
                                         scale=-1.0, bias=1.0)
                    ins = nc.scalar.activation(mT_by[half, 1, 0:T // 2, :], neT_ps[W:P, 0:T // 2, :], ACT.Copy,
                                               scale=-1.0, bias=1.0)
                ins.then_inc(mT_ready, 1)

            def u_high(s):
                nc.scalar.copy(u_parts[:, 0:UC], u_win[s][:, 0:UC]).then_inc(high_ready, 1)

            def u_middle(n1):
                act.wait_ge(rest_ready, n1)
                nc.scalar.copy(u_parts[W:P, 0:UC], u_rest[W:P, :])
                nc.scalar.copy(u_mid[:], u_rest[0:W, :]).then_inc(mid_ready, 1)

            def copy_sums(k, n1):
                act.wait_ge(agg_done, n1)
                nc.scalar.copy(state[k][0:W, 0:UC], agg).then_inc(sums_copied, 1)

            def factor(m, n1):
                act.wait_ge(mdif_ready, n1)
                nc.scalar.activation(m_fac[0:m, :], m_dif[0:m, :], ACT.Exp).then_inc(mfac_ready, 1)

            def exponentials(n1):
                act.wait_ge(shifted, n1)
                nc.scalar.activation(prob[:], score[:], ACT.Exp).then_inc(prob_ready, 1)

            def copy_aggT(n1):
                act.wait_ge(aggT_done, n1)
                nc.scalar.copy(aggT[:], aggT_ps).then_inc(aggT_ready, 1)

            def inverse_std(n1, mv_done, ln_done, done):
                act.wait_ge(mv_done, n1)
                nc.scalar.activation(lnv[:], mv[:, 1:2], ACT.Ln, bias=eps_t[0:W, :]).then_inc(ln_done, 1)
                act.wait_ge(ln_done, n1)
                nc.scalar.activation(rstd[:], lnv[:], ACT.Exp, scale=-0.5).then_inc(done, 1)

            def node_std(n1, c1, last):
                if last:
                    act.wait_ge(mneg_ready, c1)
                    nc.scalar.activation(ex[:], xr[:], ACT.Exp, bias=mneg[:], accum_out=esum[:]).then_inc(ex_ready, 1)
                    act.wait_ge(ex_ready, c1)
                    nc.scalar.activation(lse[:], esum[:], ACT.Ln).then_inc(lse_ready, 1)
                else:
                    inverse_std(n1, mv_ready, lnv_ready, rstd_ready)

            def node_copies(s, n1, last, ending=False):
                if ending and not last:
                    act.wait_ge(u_stored, 16 * (n1 - SLOTS + U0N))
                    act.sem_inc(act_mark, 1)
                if not last:
                    act.wait_ge(xnT_done, n1)
                    nc.scalar.copy(xnT[0:D, :], xnT_ps).then_inc(xnT_ready, 1)
                    act.wait_ge(uo_done, n1)
                    nc.scalar.copy(u_out[s][:], uo_ps).then_inc(uo_ready, 1)

            def layer_weights(l, last):
                nc.scalar.copy(ve_cur[:], ve_all[:, bass.ds(l, 1), :].rearrange("p a d -> p (a d)"))
                ins = nc.scalar.copy(vec_cur[:], vec_all[:, bass.ds(l, 1), :].rearrange("p a d -> p (a d)"))
                if not last:
                    ins = nc.scalar.copy(g_next[:], g_all[:, bass.ds(l + 1, 1), :].rearrange("p a d -> p (a d)"))
                ins.then_inc(layer_w, 1)

            def chunk(l, c, g1, s, last, before, more2, ending=False):
                n = act.snap(l * C + c)
                n1 = act.snap(n + 1)
                if before:
                    copy_sums(1 - s % 2, n)
                act.wait_ge(old_done, n1)
                nc.scalar.copy(old[:], old_ps).then_inc(old_ready, 1)
                if before:
                    copy_aggT(n)
                factor(1, n1)
                exponentials(n1)
                if before:
                    node_std(n, c, last)
                if more2:
                    act.wait_ge(uwin_loaded[(s + 2) % SLOTS], 32 * (g1 + 1 if s >= SLOTS - 2 else g1))
                    act.wait_ge(u_gathered, n + 2)
                    u_high((s + 2) % SLOTS)
                    mask_rows(n + 3)
                    u_middle(n + 3)
                if before and last:
                    inverse_std(c, res_mv, res_lnv, res_rstd)
                if before:
                    node_copies((s - 1) % SLOTS, n, last, ending)

            def sorted_layer(l, last):
                act.wait_ge(uwin_loaded[0], 32 * (l * GROUPS + 1))
                u_high(0)
                u_middle(l * C + 1)
                mask_rows(l * C + 1)
                layer_weights(l, last)
                act.wait_ge(uwin_loaded[1], 32 * (l * GROUPS + 1))
                act.wait_ge(u_gathered, l * C + 1)
                u_high(1)
                mask_rows(l * C + 2)
                u_middle(l * C + 2)
                for s in range(SLOTS):
                    chunk(l, s, l * GROUPS + 1, s, last, s > 0, True)
                with act.Fori(1, GROUPS - 1) as g:
                    g1 = act.snap(l * GROUPS + g + 1)
                    for s in range(SLOTS):
                        chunk(l, g * SLOTS + s, g1, s, last, True, True)
                for s in range(SLOTS):
                    chunk(l, C - SLOTS + s, l * GROUPS + GROUPS, s, last, True, s < SLOTS - 2, True)
                n = act.snap(l * C + C)
                copy_sums(1, n)
                copy_aggT(n)
                node_std(n, C, last)
                if last:
                    inverse_std(C, res_mv, res_lnv, res_rstd)
                node_copies(SLOTS - 1, n, last, True)

            def general_layer(l, last):
                layer_weights(l, last)
                with act.Fori(0, C * NWIN) as j:
                    n1 = act.snap(l * (C * NWIN) + j + 1)
                    act.wait_ge(win_loaded, l * STEPS + j + 1)
                    u_high(0)
                    u_middle(n1)
                    mask_rows(n1)
                    factor(W, n1)
                    exponentials(n1)
                    copy_sums(0, n1)
                with act.Fori(0, NWIN) as w:
                    n1 = act.snap(l * NWIN + w + 1)
                    copy_aggT(n1)
                    node_std(n1, w + 1, last)
                    if last:
                        inverse_std(w + 1, res_mv, res_lnv, res_rstd)
                    node_copies(0, n1, last)

            act.wait_ge(flag_ready, 1)
            general = act.value_load(flag_i[:], min_val=0, max_val=1)
            with act.If(general):
                with act.Fori(0, L - 1) as l:
                    general_layer(l, False)
                general_layer(L - 1, True)
            with act.Else():
                with act.Fori(0, L - 1) as l:
                    sorted_layer(l, False)
                sorted_layer(L - 1, True)

        @block.vector
        def _(dve):
            nc.vector.memset(ones[:], 1.0)
            nc.vector.memset(eps_t[:], LN_EPS)
            nc.vector.memset(xnT[D:D + 1, :], 1.0)
            nc.vector.memset(u_parts[W:P, UC:2 * UC], 0.0)
            nc.vector.memset(xT1[D:D + 1, :], 1.0)
            for s in range(SLOTS):
                nc.vector.memset(feat[s][:, :, F2:UC], 1.0)
            for k in range(2):
                nc.vector.memset(state[k][:, 0:UC], 0.0)
                ins = nc.vector.memset(state[k][:, UC:SC], M_INIT)
            ins.then_inc(const_ready, 1)
            dve.wait_ge(src_loaded, 16)
            for s in range(SLOTS):
                nc.vector.tensor_copy(idx[s][:], src_l[:, s * T:(s + 1) * T]).then_inc(idx_ready, 1)
            for l in range(1, L):
                nc.vector.tensor_scalar(src_l[:, l * C * T:(l + 1) * C * T], src_l[:, 0:C * T], float((l - 1) * NP), None, ALU.add)
            nc.vector.tensor_copy(src_l[:, L * C * T:], src_l[:, 0:SLOTS * T])
            dve.wait_ge(dst_loaded, 16)
            nc.vector.tensor_copy(dst_f[:], dst_i[:]).then_inc(dst_ready, 1)
            dve.wait_ge(iota_ready, 2)
            nc.vector.tensor_copy(iota_w, iota_i[:, 0:W])
            nc.vector.tensor_scalar(wbase[:], iota_i[:, 0:NWIN], float(W), None, ALU.mult)
            nc.vector.tensor_scalar(row_id[:], diag_i[:, 0:1], -1.0, None, ALU.mult)
            nc.vector.tensor_scalar(ident[:], diag_i[:], 0.0, None, ALU.is_equal)
            nc.vector.tensor_scalar(ident_b[:], diag_i[:], 0.0, None, ALU.is_equal).then_inc(const_ready, 1)
            dve.wait_ge(const_ready, 2)
            dve.wait_ge(base_mm, 1)
            nc.vector.tensor_copy(base_b[:], max_ps[:, 0:C + 1]).then_inc(base_ready, 1)
            dve.wait_ge(base_ready, 1)
            nc.vector.memset(step_b[:, 0:1], float(W))
            nc.vector.tensor_tensor(step_b[:, 1:C], base_b[:, 1:C], base_b[:, 0:C - 1], ALU.subtract).then_inc(test_step, 1)
            dve.wait_ge(test_step, 1)
            nc.vector.tensor_scalar(sel_all[:], step_b[0:W + 1, :], row_id[0:W + 1, :], None, ALU.is_equal)
            nc.vector.memset(lim[:, C - 1:C], float(W - 1))
            nc.vector.tensor_scalar(lim[:, 0:C - 1], step_b[:, 1:C], float(W - 1), None, ALU.min).then_inc(test_step, 1)
            full = dst_f[:, 0:C * T].rearrange("p (c t) -> p c t", t=T)
            nc.vector.tensor_tensor(far[:], full, base_b[:, 0:C].unsqueeze(2).to_broadcast([P, C, T]),
                                    ALU.subtract).then_inc(test_step, 1)
            dve.wait_ge(test_step, 3)
            nc.vector.tensor_tensor(wide[:], far[:], lim[:].unsqueeze(2).to_broadcast([P, C, T]), ALU.is_gt).then_inc(test_step, 1)
            dve.wait_ge(test_step, 4)
            nc.vector.scalar_tensor_tensor(wide[:], full, float(PAD_DST), wide[:], ALU.is_lt, ALU.mult).then_inc(test_step, 1)
            dve.wait_ge(test_step, 5)
            nc.vector.scalar_tensor_tensor(wide[:], far[:], 0.0, wide[:], ALU.is_lt, ALU.add).then_inc(test_step, 1)
            dve.wait_ge(test_step, 6)
            nc.vector.tensor_reduce(bad[:, 0:1], wide[:], AX.XY, ALU.add)
            nc.vector.tensor_scalar(lim[:], step_b[:], float(W), None, ALU.is_gt).then_inc(test_step, 1)
            nc.vector.tensor_scalar(bad[:, 2:3], base_b[:, 0:1], 0.0, float(FORCE_GENERAL), ALU.is_gt, ALU.add)
            nc.vector.tensor_scalar(bad[:, 3:4], base_b[:, C - 1:C], float(N - W), None, ALU.is_lt)
            dve.wait_ge(test_step, 7)
            nc.vector.tensor_reduce(bad[:, 1:2], lim[:], AX.X, ALU.add).then_inc(test_step, 1)
            dve.wait_ge(test_step, 8)
            nc.vector.tensor_reduce(bad_n[:], bad[:], AX.X, ALU.add).then_inc(bad_ready, 1)
            dve.wait_ge(bad_mm, 1)
            nc.vector.tensor_scalar(flag_f[:], max_ps[0:1, 256:257], 1.0, None, ALU.min).then_inc(test_step, 1)
            dve.wait_ge(test_step, 9)
            nc.vector.tensor_copy(flag_i[:], flag_f[:]).then_inc(flag_ready, 1)

            def node_mask(c, base, k, n1):
                nc.vector.tensor_scalar(rel[k][:], dst_f[:, bass.ds(c * T, T)], base, None, ALU.subtract).then_inc(rel_ready, 1)
                dve.wait_ge(rel_ready, n1)
                nc.vector.tensor_tensor(ne[k][:], rel[k][:].unsqueeze(2).to_broadcast([P, T, W]),
                                        iota_w.unsqueeze(1).to_broadcast([P, T, W]), ALU.not_equal).then_inc(ne_ready, 1)

            def u_remainder(s, n1):
                dve.wait_ge(high_ready, n1)
                nc.vector.tensor_tensor(u_rest[:], u_win[s][:, 0:UC], u_parts[:, 0:UC], ALU.subtract).then_inc(rest_ready, 1)

            def u_last(n1):
                dve.wait_ge(mid_ready, n1)
                nc.vector.tensor_tensor(u_parts[0:W, UC:2 * UC], u_rest[0:W, :], u_mid[:], ALU.subtract).then_inc(parts_ready, 1)

            def scores(s, g1, n1):
                dve.wait_ge(u_gathered, n1)
                dve.wait_ge(edge_loaded[s], 16 * g1)
                dve.wait_ge(rows_loaded[s], (16 * T_FIRST) * g1)
                for t in range(T):
                    if t == T_FIRST:
                        dve.wait_ge(rest_loaded[s], (16 * (T - T_FIRST)) * g1)
                    ins = nc.vector.tensor_tensor_reduce(dot_out[:, t, :], feat[s][:, t, 0:UC], u_slot(t), 1.0, 0.0,
                                                         ALU.mult, ALU.add, alpha[:, t:t + 1])
                ins.then_inc(dots_done, 1)

            def maxima(k, n1):
                dve.wait_ge(dots_done, n1)
                nc.vector.scalar_tensor_tensor(score[:], ne[k][:], -BIG, alpha[:].unsqueeze(2).to_broadcast([P, T, W]),
                                               ALU.mult, ALU.add).then_inc(score_ready, 1)
                dve.wait_ge(score_ready, n1)
                nc.vector.tensor_reduce(cmax[:], score[:].rearrange("p t n -> p n t"), AX.X, ALU.max).then_inc(cmax_ready, 1)

            def subtract_max(n1):
                dve.wait_ge(m_bc_done, n1)
                nc.vector.tensor_tensor(score[:], score[:], m_bc.unsqueeze(1).to_broadcast([P, T, W]),
                                        ALU.subtract).then_inc(shifted, 1)

            def node_inverse(k, s, n1):
                nc.vector.tensor_scalar(d_pos[:], state[k][0:W, F2:UC], 1e-30, None, ALU.max).then_inc(dpos_ready, 1)
                dve.wait_ge(dpos_ready, n1)
                nc.vector.reciprocal(d_inv[:], d_pos[:]).then_inc(dinv_ready, 1)
                dve.wait_ge(dinv_ready, n1)
                nc.vector.tensor_tensor(some[:], state[k][0:W, F2:UC], d_inv[:], ALU.mult).then_inc(some_ready, 1)
                dve.wait_ge(some_ready, n1)
                nc.vector.scalar_tensor_tensor(skip[:], vec_cur[:, 0:D], some[:], u_win[s][0:W, UC:UW], ALU.mult,
                                               ALU.add).then_inc(skip_ready, 1)

            def node_out(n1, c1, last):
                dve.wait_ge(o_done, n1)
                dve.wait_ge(skip_ready, n1)
                nc.vector.scalar_tensor_tensor(xo[:], o_ps, d_inv[:], skip[:], ALU.mult, ALU.add).then_inc(xo_ready, 1)
                dve.wait_ge(xo_ready, n1)
                nc.vector.tensor_scalar(xr[:], xo[:], 0.0, None, ALU.max).then_inc(xr_ready, 1)
                dve.wait_ge(xr_ready, n1)
                if last:
                    nc.vector.tensor_reduce(mx[:], xr[:], AX.X, ALU.max).then_inc(mx_ready, 1)
                    dve.wait_ge(mx_ready, c1)
                    nc.vector.tensor_scalar(mneg[:], mx[:], -1.0, None, ALU.mult).then_inc(mneg_ready, 1)
                else:
                    nc.vector.bn_stats(bns[:], xr[:]).then_inc(bns_ready, 1)
                    dve.wait_ge(bns_ready, n1)
                    dve.sem_inc(dve_mark, 1)
                    nc.vector.bn_aggr(mv[:], bns[:]).then_inc(mv_ready, 1)

            def node_norm(s, n1, c1, last, x0_here=None, ending=False):
                if ending and not last:
                    dve.wait_ge(x_stored, 16 * (n1 - SLOTS))
                    dve.sem_inc(dve_mark, 1)
                if last:
                    dve.wait_ge(lse_ready, c1)
                    nc.vector.tensor_tensor(shift[:], mx[:], lse[:], ALU.add).then_inc(shift_ready, 1)
                    if x0_here is not None:
                        dve.wait_ge(x0_loaded[s], x0_here)
                    dve.wait_ge(shift_ready, c1)
                    nc.vector.scalar_tensor_tensor(xn[:], xr[:], shift[:], x0[s][:], ALU.subtract,
                                                   ALU.add).then_inc(logp_ready, 1)
                    dve.wait_ge(logp_ready, c1)
                    nc.vector.bn_stats(bns[:], xn[:]).then_inc(res_bns, 1)
                    dve.wait_ge(res_bns, c1)
                    dve.sem_inc(dve_mark, 1)
                    nc.vector.bn_aggr(mv[:], bns[:]).then_inc(res_mv, 1)
                else:
                    dve.wait_ge(mv_ready, n1)
                    nc.vector.scalar_tensor_tensor(xn[:], xr[:], mv[:, 0:1], vec_cur[:, D:2 * D], ALU.subtract,
                                                   ALU.mult).then_inc(xn_ready, 1)
                    dve.wait_ge(rstd_ready, n1)
                    dve.wait_ge(xn_ready, n1)
                    nc.vector.scalar_tensor_tensor(xnew[s][:], xn[:], rstd[:], vec_cur[:, 2 * D:3 * D], ALU.mult,
                                                   ALU.add).then_inc(xnew_ready, 1)

            def node_final(s, c1, ending=False):
                if ending:
                    dve.wait_ge(out_stored, 16 * (c1 - SLOTS))
                    dve.sem_inc(dve_mark, 1)
                dve.wait_ge(res_rstd, c1)
                nc.vector.tensor_scalar(xnew[s][:], xn[:], mv[:, 0:1], rstd[:], ALU.subtract, ALU.mult).then_inc(res_ready, 1)

            def merge(k, n1):
                dve.wait_ge(sums_copied, n1)
                dve.wait_ge(mfac_ready, n1)
                nc.vector.scalar_tensor_tensor(state[k][0:1, 0:UC], old[:, 0:UC], m_fac[0:1, :], state[k][0:1, 0:UC],
                                               ALU.mult, ALU.add).then_inc(merged, 1)

            def chunk(l, c, g1, s, last, before, before2, more, more2, ending=False):
                n = dve.snap(l * C + c)
                n1 = dve.snap(n + 1)
                k = s % 2
                ps = (s - 1) % SLOTS
                scores(s, g1, n1)
                if more:
                    u_last(n + 2)
                if before2 and last:
                    node_final((s - 2) % SLOTS, c - 1, ending)
                nc.vector.tensor_copy(idx[s][:], src_l[:, bass.ds((n + SLOTS) * T, T)]).then_inc(idx_ready, 1)
                if before:
                    dve.wait_ge(prob_ready, n)
                maxima(k, n1)
                if before:
                    merge(1 - k, n)
                nc.vector.tensor_copy(sel[:], sel_all[:, bass.ds(c, 1)]).then_inc(sel_ready, 1)
                dve.wait_ge(cmT_done, n1)
                nc.vector.tensor_reduce(cm[:], cmT, AX.X, ALU.max).then_inc(cm_ready, 1)
                if before:
                    dve.wait_ge(merged, n)
                    node_inverse(1 - k, ps, n)
                dve.wait_ge(cm_ready, n1)
                dve.wait_ge(old_ready, n1)
                nc.vector.tensor_tensor(cm[0:1, :], cm[0:1, :], old[:, UC:SC], ALU.max).then_inc(m_ready, 1)
                dve.wait_ge(m_ready, n1)
                nc.vector.tensor_scalar(diag[:], ident[0:W, 0:W], cm[:], M_INIT, ALU.mult, ALU.max).then_inc(diag_ready, 1)
                nc.vector.tensor_tensor(m_dif[0:1, :], old[:, UC:SC], cm[0:1, :], ALU.subtract).then_inc(mdif_ready, 1)
                nc.vector.tensor_scalar(state[k][0:W, UC:SC], cm[:], M_INIT, None, ALU.max)
                subtract_max(n1)
                if before:
                    node_out(n, c, last)
                if more2:
                    node_mask(c + 2, base_b[:, bass.ds(c + 2, 1)], k, n + 3)
                    u_remainder((s + 2) % SLOTS, n + 3)
                if before:
                    node_norm(ps, n, c, last, 16 * (g1 - (L - 1) * GROUPS - (s == 0)) if last else None, ending)

            def sorted_layer(l, last):
                n0 = dve.snap(l * C)
                node_mask(0, base_b[:, 0:1], 0, n0 + 1)
                node_mask(1, base_b[:, 1:2], 1, n0 + 2)
                u_remainder(0, n0 + 1)
                u_last(n0 + 1)
                u_remainder(1, n0 + 2)
                dve.wait_ge(layer_w, l + 1)
                dve.sem_inc(dve_mark, 1)
                for s in range(SLOTS):
                    chunk(l, s, l * GROUPS + 1, s, last, s > 0, s > 1, True, True)
                with dve.Fori(1, GROUPS - 1) as g:
                    g1 = dve.snap(l * GROUPS + g + 1)
                    for s in range(SLOTS):
                        chunk(l, g * SLOTS + s, g1, s, last, True, True, True, True)
                for s in range(SLOTS):
                    chunk(l, C - SLOTS + s, l * GROUPS + GROUPS, s, last, True, True, s < SLOTS - 1, s < SLOTS - 2, True)
                n = dve.snap(l * C + C)
                if last:
                    node_final(SLOTS - 2, C - 1, True)
                merge(1, n)
                dve.wait_ge(merged, n)
                node_inverse(1, SLOTS - 1, n)
                node_out(n, C, last)
                node_norm(SLOTS - 1, n, C, last, 16 * GROUPS if last else None, True)
                if last:
                    node_final(SLOTS - 1, C, True)

            def general_step(l, c, g1, s, w):
                n1 = dve.snap(l * (C * NWIN) + c * NWIN + w + 1)
                m_old = all_flat[:, bass.ds(w * SC + UC, 1)]
                sums = all_flat[:, bass.ds(w * SC, UC)]
                node_mask(c, wbase[:, bass.ds(w, 1)], 0, n1)
                u_remainder(0, n1)
                u_last(n1)
                scores(s, g1, n1)
                maxima(0, n1)
                dve.wait_ge(cmT_done, n1)
                nc.vector.tensor_reduce(cm[:], cmT, AX.X, ALU.max).then_inc(cm_ready, 1)
                dve.wait_ge(cm_ready, n1)
                nc.vector.tensor_tensor(m_new[:], cm[:], m_old, ALU.max).then_inc(m_ready, 1)
                dve.wait_ge(m_ready, n1)
                nc.vector.tensor_scalar(diag[:], ident[0:W, 0:W], m_new[:], None, ALU.mult).then_inc(diag_ready, 1)
                nc.vector.tensor_tensor(m_dif[:], m_old, m_new[:], ALU.subtract).then_inc(mdif_ready, 1)
                subtract_max(n1)
                dve.wait_ge(sums_copied, n1)
                dve.wait_ge(mfac_ready, n1)
                nc.vector.scalar_tensor_tensor(sums, sums, m_fac[:], state[0][0:W, 0:UC], ALU.mult, ALU.add)
                nc.vector.tensor_copy(m_old, m_new[:]).then_inc(window_merged, 1)
                dve.wait_ge(window_merged, n1)

            def general_layer(l, last):
                dve.wait_ge(layer_w, l + 1)
                nc.vector.memset(all_flat, 0.0).then_inc(state_set, 1)
                dve.wait_ge(state_set, 2 * l + 1)
                nc.vector.memset(all_state[:, :, UC:SC], M_INIT).then_inc(state_set, 1)
                dve.wait_ge(state_set, 2 * l + 2)
                dve.sem_inc(dve_mark, 1)
                with dve.Fori(0, GROUPS) as g:
                    g1 = dve.snap(l * GROUPS + g + 1)
                    for s in range(SLOTS):
                        c = dve.snap(g * SLOTS + s)
                        with dve.Fori(0, NWIN) as w:
                            general_step(l, c, g1, s, w)
                        nc.vector.memset(m_dif[:], 0.0).then_inc(merged, 1)
                        dve.wait_ge(merged, l * C + c + 1)
                        nxt = dve.snap((l * C + c + SLOTS) * T)
                        nc.vector.tensor_copy(idx[s][:], src_l[:, bass.ds(nxt, T)]).then_inc(idx_ready, 1)
                with dve.Fori(0, NWIN) as w:
                    n1 = dve.snap(l * NWIN + w + 1)
                    nc.vector.tensor_copy(state[0][0:W, :], all_flat[:, bass.ds(w * SC, SC)]).then_inc(state_got, 1)
                    dve.wait_ge(state_got, n1)
                    dve.wait_ge(win_loaded, l * STEPS + C * NWIN + w + 1)
                    node_inverse(0, 0, n1)
                    node_out(n1, w + 1, last)
                    node_norm(0, n1, w + 1, last)
                    if last:
                        node_final(0, w + 1)
                    dve.wait_ge(rows_kept, n1)

            dve.wait_ge(flag_ready, 1)
            general = dve.value_load(flag_i[:], min_val=0, max_val=1)
            with dve.If(general):
                dve.wait_ge(u_stored, 16 * U0N)
                with dve.Fori(0, L - 1) as l:
                    general_layer(l, False)
                general_layer(L - 1, True)
            with dve.Else():
                with dve.Fori(0, L - 1) as l:
                    sorted_layer(l, False)
                sorted_layer(L - 1, True)

        @block.tensor
        def _(pe):
            pe.sem_inc(win_free, 1)
            pe.wait_ge(const_ready, 1)
            pe.wait_ge(dst_ready, 1)
            firsts = dst_f[0:1, :].rearrange("p (c t) -> p c t", t=T)[:, :, 0]
            nc.tensor.matmul(max_ps[:, 0:C + 1], ones[0:1, :], firsts, start=True, stop=True).then_inc(base_mm, 1)
            pe.wait_ge(weights_loaded, 16 * N_WEIGHTS)
            for l in range(L):
                nc.tensor.matmul(u_ps[0:D + 1, l, 0:UC], qT_sb[:, l, :], ke_sb[:, l, :], start=True, stop=True).then_inc(g_mm, 1)
            pe.wait_ge(g_ready, L)
            for i in range(U0N):
                if i >= 2:
                    pe.wait_ge(u0_copied, i - 1)
                for b in range(U0B):
                    r = (i * U0B + b) * P
                    ins = nc.tensor.matmul(u_ps[:, 2 * (i % 2) + b // 2, (b % 2) * 256:(b % 2) * 256 + UW], xT1[:, r:r + P],
                                           g_all[:, 0, :], start=True, stop=True)
                ins.then_inc(u0_mm, 1)
                if i == U0_FIRST - 1:
                    pe.wait_ge(bad_ready, 1)
                    pe.wait_ge(base_ready, 1)
                    nc.tensor.matmul(max_ps[0:1, 256:257], bad_n[:], ones[:, 0:1], start=True, stop=True).then_inc(bad_mm, 1)

            def turn_mask(k, n1):
                pe.wait_ge(ne_ready, n1)
                for t in range(0, T, 2):
                    w = min(2, T - t) * W
                    ins = nc.tensor.transpose(neT_ps[0:w, t // 2, :], ne[k][:, t:t + w // W, :].rearrange("p t n -> p (t n)"),
                                              ident_b[:])
                ins.then_inc(neT_done, 1)

            def gather_u(n1):
                pe.wait_ge(mT_ready, n1)
                pe.wait_ge(parts_ready, n1)
                for t in range(T):
                    nc.tensor.matmul(u_slot(t), mT[:, t, :], u_parts[:, 0:UC], start=True, stop=False)
                    ins = nc.tensor.matmul(u_slot(t), mT[:, t, :], u_parts[:, UC:2 * UC], start=False, stop=True)
                ins.then_inc(u_gathered, 1)

            def turn_max(n1):
                pe.wait_ge(cmax_ready, n1)
                pe.sem_inc(pe_mark, 1)
                nc.tensor.transpose(cmT, cmax[:], ident[:]).then_inc(cmT_done, 1)

            def spread_max(n1):
                pe.wait_ge(diag_ready, n1)
                nc.tensor.matmul(m_bc, ones[0:W, :], diag[:], start=True, stop=True).then_inc(m_bc_done, 1)

            def sums(s, n1):
                pe.wait_ge(prob_ready, n1)
                for t in range(T):
                    ins = nc.tensor.matmul(agg, prob[:, t, :], feat[s][:, t, 0:UC], start=(t == 0), stop=(t == T - 1))
                ins.then_inc(agg_done, 1)

            def turn_sums(k):
                nc.tensor.transpose(aggT_ps, state[k][0:W, 0:F2], ident[0:W, 0:W]).then_inc(aggT_done, 1)

            def node_product(n1):
                pe.wait_ge(aggT_ready, n1)
                nc.tensor.matmul(o_ps, aggT[:], ve_cur[:], start=True, stop=True).then_inc(o_done, 1)

            def node_rows(s, n1):
                pe.wait_ge(xnew_ready, n1)
                pe.sem_inc(pe_mark, 1)
                nc.tensor.transpose(xnT_ps, xnew[s][:], ident[0:W, 0:W]).then_inc(xnT_done, 1)
                pe.wait_ge(xnT_ready, n1)
                nc.tensor.matmul(uo_ps, xnT[:], g_next[:], start=True, stop=True).then_inc(uo_done, 1)

            def chunk(l, c, s, last, before, more, more2):
                n = pe.snap(l * C + c)
                n1 = pe.snap(n + 1)
                k = s % 2
                turn_max(n1)
                if before:
                    pe.wait_ge(merged, n)
                    pe.sem_inc(pe_mark, 1)
                    turn_sums(1 - k)
                pe.wait_ge(sel_ready, n1)
                pe.sem_inc(pe_mark, 1)
                nc.tensor.matmul(old_ps, sel[:], state[1 - k][:], start=True, stop=True).then_inc(old_done, 1)
                spread_max(n1)
                if before:
                    node_product(n)
                if more:
                    gather_u(n + 2)
                if more2:
                    turn_mask(k, n + 3)
                if before:
                    pe.wait_ge(xo_ready, n)
                    pe.sem_inc(pe_mark, 1)
                sums(s, n1)
                if before and not last:
                    node_rows((s - 1) % SLOTS, n)
                    pe.wait_ge(uo_ready, n)
                    pe.sem_inc(pe_mark, 1)

            def sorted_layer(l, last):
                pe.wait_ge(ne_ready, l * C + 2)
                pe.sem_inc(pe_mark, 1)
                turn_mask(0, l * C + 1)
                gather_u(l * C + 1)
                turn_mask(1, l * C + 2)
                pe.wait_ge(layer_w, l + 1)
                pe.sem_inc(pe_mark, 1)
                for s in range(SLOTS):
                    chunk(l, s, s, last, s > 0, True, True)
                with pe.Fori(1, GROUPS - 1) as g:
                    for s in range(SLOTS):
                        chunk(l, g * SLOTS + s, s, last, True, True, True)
                for s in range(SLOTS):
                    chunk(l, C - SLOTS + s, s, last, True, s < SLOTS - 1, s < SLOTS - 2)
                n = pe.snap(l * C + C)
                pe.wait_ge(merged, n)
                pe.sem_inc(pe_mark, 1)
                turn_sums(1)
                node_product(n)
                if not last:
                    node_rows(SLOTS - 1, n)
                    pe.wait_ge(uo_ready, n)

            def general_layer(l, last):
                pe.wait_ge(layer_w, l + 1)
                pe.sem_inc(pe_mark, 1)
                with pe.Fori(0, GROUPS) as g:
                    for s in range(SLOTS):
                        with pe.Fori(0, NWIN) as w:
                            j = pe.snap((g * SLOTS + s) * NWIN + w)
                            n1 = pe.snap(l * (C * NWIN) + j + 1)
                            turn_mask(0, n1)
                            gather_u(n1)
                            turn_max(n1)
                            spread_max(n1)
                            sums(s, n1)
                            pe.wait_ge(window_merged, n1)
                            pe.sem_inc(win_free, 1)
                with pe.Fori(0, NWIN) as w:
                    n1 = pe.snap(l * NWIN + w + 1)
                    pe.wait_ge(state_got, n1)
                    pe.sem_inc(pe_mark, 1)
                    turn_sums(0)
                    node_product(n1)
                    if not last:
                        node_rows(0, n1)
                        pe.wait_ge(uo_ready, n1)
                    pe.wait_ge(rows_kept, n1)
                    pe.sem_inc(win_free, 1)

            pe.wait_ge(flag_ready, 1)
            general = pe.value_load(flag_i[:], min_val=0, max_val=1)
            with pe.If(general):
                with pe.Fori(0, L - 1) as l:
                    general_layer(l, False)
                general_layer(L - 1, True)
            with pe.Else():
                with pe.Fori(0, L - 1) as l:
                    sorted_layer(l, False)
                sorted_layer(L - 1, True)


def kernel(**inputs):
    import numpy as np
    import concourse.bacc as bacc
    from concourse.bass_utils import run_bass_kernel_spmd

    a = {k.replace("L0_gnn_", ""): np.asarray(v) for k, v in inputs.items()}

    def chunked(edges, fill):
        full = np.concatenate([edges, np.full(C * EC - E, fill, edges.dtype)])
        return full.reshape(C, P, T).transpose(1, 0, 2)

    x_rows = np.concatenate([a["x"], np.zeros((NP - N, D), a["x"].dtype)])
    dst = chunked(a["dst"], PAD_DST)
    ea = a["edge_attr_64"]
    none = np.zeros((1, D), a["ln_gamma"].dtype)
    vec = np.concatenate([a["bv"], np.concatenate([a["ln_gamma"], none]), np.concatenate([a["ln_beta"], none])], 1)
    arrays = {
        "x": x_rows,
        "xT": x_rows.T,
        "src": chunked(a["src"], 0).reshape(P, C * T),
        "dst": np.concatenate([dst, dst[:, 0:1]], 1).reshape(P, (C + 1) * T),
        "edge": np.concatenate([ea, np.zeros((C * EC - E, D), ea.dtype)]).reshape(C, P, T * D),
        "w_qT": np.concatenate([a["Wq"], a["bq"][:, None, :]], 1).transpose(2, 0, 1),
        "w_ke": np.concatenate([a["Wk"].transpose(0, 2, 1), a["We"].transpose(0, 2, 1), a["bk"][:, :, None]], 2).transpose(1, 0, 2),
        "w_sk": np.concatenate([a["Ws"], a["bs"][:, None, :]], 1).transpose(1, 0, 2),
        "w_ve": np.concatenate([a["Wv"], a["We"]], 1).transpose(1, 0, 2),
        "w_vec": np.broadcast_to(vec[None], (W, L, 3 * D)),
    }
    arrays = {k: np.ascontiguousarray(v) for k, v in arrays.items()}
    nc = bacc.Bacc("TRN2", target_bir_lowering=False, num_devices=1)
    aps = {k: nc.dram_tensor(k, v.shape, mybir.dt.from_np(v.dtype), kind="ExternalInput").ap() for k, v in arrays.items()}
    aps["out"] = nc.dram_tensor("out", (NP, D), F32, kind="ExternalOutput").ap()
    aps["x_table"] = nc.dram_tensor("x_table", ((L - 1) * NP, D), F32, kind="Internal").ap()
    aps["u_table"] = nc.dram_tensor("u_table", (L * NP, UW), F32, kind="Internal").ap()
    gnn_kernel(nc, **aps)
    r = run_bass_kernel_spmd(nc, [arrays], core_ids=[0])
    return r.results[0]["out"][:N]
```
